# Optimizing a Trainium2 kernel written in Bass

```python
import numpy as np
import jax
import jax.numpy as jnp

def _softmax(x, axis=-1):
    return jax.nn.softmax(x, axis=axis)

def _gelu(x):
    return jax.nn.gelu(x, approximate=True)

def _silu(x):
    return jax.nn.silu(x)

def _sigmoid(x):
    return jax.nn.sigmoid(x)

def _layernorm(x, axis=-1, eps=1e-05):
    m = jnp.mean(x, axis=axis, keepdims=True)
    v = jnp.var(x, axis=axis, keepdims=True)
    return (x - m) / jnp.sqrt(v + eps)

def _scatter_add(tgt, idx, src, axis=0):
    return tgt.at[idx].add(src)

def _segment_sum(src, seg, n):
    return jax.ops.segment_sum(src, seg, n)
kernel_name = 'mk_gnn_resnorm_d1_gnn_r32_f2fc92'

def setup_inputs(seed: int=0):
    np.random.seed(seed)
    _w = jnp.asarray

    def _rec_inputs():
        import jax
        import jax.numpy as jnp
        _gk = jax.random.key(seed)
        x = -0.000202 + 1 * jax.random.normal(jax.random.fold_in(_gk, 1), (3125, 160), jnp.float32)
        _s = jax.random.randint(jax.random.fold_in(_gk, 2), (50000,), 0, 3125, jnp.int32)
        _d = jax.random.randint(jax.random.fold_in(_gk, 3), (50000,), 0, 3125, jnp.int32)
        _loop = jnp.arange(3125, dtype=jnp.int32)
        src = jnp.concatenate([_s, _d, _loop])
        dst = jnp.concatenate([_d, _s, _loop])
        _o = jnp.argsort(dst, stable=True)
        src = src[_o]
        dst = dst[_o]
        edge_attr_4 = 0.0012443 + 1.0001 * jax.random.normal(jax.random.fold_in(_gk, 12), (103125, 4), jnp.float32)
        edge_attr_64 = 0.000127647 + 1.00004 * jax.random.normal(jax.random.fold_in(_gk, 13), (103125, 64), jnp.float32)
        node_vec1 = jax.random.uniform(jax.random.fold_in(_gk, 14), (3125, 1), jnp.float32, 0.0, 1)
        return (x, src, dst, edge_attr_4, edge_attr_64, node_vec1)
    x, src, dst, edge_attr_4, edge_attr_64, node_vec1 = _rec_inputs()

    def _L0_gnn_setup():
        import jax, jax.numpy as jnp
        import numpy as np
        N, E = (1250, 20000)
        S_IN, V_IN = (64, 32)
        S_MID, V_MID = (96, 128)
        S_OUT, V_OUT = (96, 32)
        R = 64
        FC_HID = 64
        W_NUMEL = 64 + 64 + 32 + 32 + 32
        NUM_NEIGHBORS = 16.0

        def _inv(d):
            return 1.0 / jnp.sqrt(jnp.float32(d))

        def _forward(node_features, node_attr, edge_attr, edge_scalars, lin1_ws, lin1_wv, fc_w1, fc_w2, sc_ws, sc_wv, lin2_ws, lin2_wv, edge_src, edge_dst):
            n = node_features.shape[0]
            s = node_features[:, :S_IN]
            v = node_features[:, S_IN:].reshape(n, V_IN, 3)
            a = node_attr
            sc_s = s @ sc_ws * a * _inv(S_IN)
            sc_v = jnp.einsum('nci,cd->ndi', v, sc_wv) * a[:, :, None] * _inv(V_IN)
            h_s = s @ lin1_ws * a * _inv(S_IN)
            h_v = jnp.einsum('nci,cd->ndi', v, lin1_wv) * a[:, :, None] * _inv(V_IN)
            hid = jax.nn.silu(edge_scalars @ fc_w1 * _inv(R))
            w = hid @ fc_w2 * _inv(FC_HID)
            w1, w2, w3, w4, w5 = jnp.split(w, [64, 128, 160, 192], axis=-1)
            es = h_s[edge_src]
            ev = h_v[edge_src]
            e0 = edge_attr[:, :1]
            e1 = edge_attr[:, 1:4]
            m_s1 = w1 * es * e0
            m_s2 = w4 * jnp.einsum('eci,ei->ec', ev, e1) * _inv(3)
            m_v1 = (w2 * es)[:, :, None] * e1[:, None, :]
            m_v2 = w3[:, :, None] * ev * e0[:, :, None]
            m_v3 = w5[:, :, None] * jnp.cross(ev, e1[:, None, :]) * _inv(2)
            mid_s = jnp.concatenate([m_s1, m_s2], axis=-1)
            mid_v = jnp.concatenate([m_v1, m_v2, m_v3], axis=1)
            inv_nn = 1.0 / jnp.sqrt(jnp.float32(NUM_NEIGHBORS))
            agg_s = jax.ops.segment_sum(mid_s, edge_dst, num_segments=n) * inv_nn
            agg_v = jax.ops.segment_sum(mid_v, edge_dst, num_segments=n) * inv_nn
            o_s = agg_s @ lin2_ws * a * _inv(S_MID)
            o_v = jnp.einsum('nci,cd->ndi', agg_v, lin2_wv) * a[:, :, None] * _inv(V_MID)
            pre_s = sc_s + o_s
            pre_v = sc_v + o_v
            scalars = jax.nn.silu(pre_s[:, :64])
            gates = jax.nn.sigmoid(pre_s[:, 64:96])
            gated = gates[:, :, None] * pre_v
            return jnp.concatenate([scalars, gated.reshape(n, 3 * V_OUT)], axis=-1)
        key = jax.random.key(seed)
        ks = jax.random.split(key, 13)
        return {'node_features': jax.random.normal(ks[0], (N, S_IN + 3 * V_IN), jnp.float32), 'node_attr': jnp.ones((N, 1), jnp.float32), 'edge_src': jax.random.randint(ks[1], (E,), 0, N), 'edge_dst': jax.random.randint(ks[2], (E,), 0, N), 'edge_attr': jax.random.normal(ks[3], (E, 4), jnp.float32), 'edge_scalars': jax.random.normal(ks[4], (E, R), jnp.float32), 'lin1_ws': jax.random.normal(ks[5], (S_IN, S_IN), jnp.float32), 'lin1_wv': jax.random.normal(ks[6], (V_IN, V_IN), jnp.float32), 'fc_w1': jax.random.normal(ks[7], (R, FC_HID), jnp.float32), 'fc_w2': jax.random.normal(ks[8], (FC_HID, W_NUMEL), jnp.float32), 'sc_ws': jax.random.normal(ks[9], (S_IN, S_OUT), jnp.float32), 'sc_wv': jax.random.normal(ks[10], (V_IN, V_OUT), jnp.float32), 'lin2_ws': jax.random.normal(ks[11], (S_MID, S_OUT), jnp.float32), 'lin2_wv': jax.random.normal(ks[12], (V_MID, V_OUT), jnp.float32)}
    _L0_gnn_all = _L0_gnn_setup()
    _L0_gnn_in = {k: v for k, v in _L0_gnn_all.items() if k in ('lin1_ws', 'lin1_wv', 'fc_w1', 'fc_w2', 'sc_ws', 'sc_wv', 'lin2_ws', 'lin2_wv')}
    del _L0_gnn_all
    return {'x': x, 'src': src, 'dst': dst, 'edge_attr_4': edge_attr_4, 'edge_attr_64': edge_attr_64, 'node_vec1': node_vec1, 'L0_gnn_lin1_ws': _L0_gnn_in['lin1_ws'], 'L0_gnn_lin1_wv': _L0_gnn_in['lin1_wv'], 'L0_gnn_fc_w1': _L0_gnn_in['fc_w1'], 'L0_gnn_fc_w2': _L0_gnn_in['fc_w2'], 'L0_gnn_sc_ws': _L0_gnn_in['sc_ws'], 'L0_gnn_sc_wv': _L0_gnn_in['sc_wv'], 'L0_gnn_lin2_ws': _L0_gnn_in['lin2_ws'], 'L0_gnn_lin2_wv': _L0_gnn_in['lin2_wv']}

def reference(x, src, dst, edge_attr_4, edge_attr_64, node_vec1, L0_gnn_lin1_ws, L0_gnn_lin1_wv, L0_gnn_fc_w1, L0_gnn_fc_w2, L0_gnn_sc_ws, L0_gnn_sc_wv, L0_gnn_lin2_ws, L0_gnn_lin2_wv):
    import jax
    import jax.numpy as jnp

    def _L0_gnn_ref(node_features, node_attr, edge_src, edge_dst, edge_attr, edge_scalars, lin1_ws, lin1_wv, fc_w1, fc_w2, sc_ws, sc_wv, lin2_ws, lin2_wv):
        import jax, jax.numpy as jnp
        import numpy as np
        N, E = (1250, 20000)
        S_IN, V_IN = (64, 32)
        S_MID, V_MID = (96, 128)
        S_OUT, V_OUT = (96, 32)
        R = 64
        FC_HID = 64
        W_NUMEL = 64 + 64 + 32 + 32 + 32
        NUM_NEIGHBORS = 16.0

        def _inv(d):
            return 1.0 / jnp.sqrt(jnp.float32(d))

        def _forward(node_features, node_attr, edge_attr, edge_scalars, lin1_ws, lin1_wv, fc_w1, fc_w2, sc_ws, sc_wv, lin2_ws, lin2_wv, edge_src, edge_dst):
            n = node_features.shape[0]
            s = node_features[:, :S_IN]
            v = node_features[:, S_IN:].reshape(n, V_IN, 3)
            a = node_attr
            sc_s = s @ sc_ws * a * _inv(S_IN)
            sc_v = jnp.einsum('nci,cd->ndi', v, sc_wv) * a[:, :, None] * _inv(V_IN)
            h_s = s @ lin1_ws * a * _inv(S_IN)
            h_v = jnp.einsum('nci,cd->ndi', v, lin1_wv) * a[:, :, None] * _inv(V_IN)
            hid = jax.nn.silu(edge_scalars @ fc_w1 * _inv(R))
            w = hid @ fc_w2 * _inv(FC_HID)
            w1, w2, w3, w4, w5 = jnp.split(w, [64, 128, 160, 192], axis=-1)
            es = h_s[edge_src]
            ev = h_v[edge_src]
            e0 = edge_attr[:, :1]
            e1 = edge_attr[:, 1:4]
            m_s1 = w1 * es * e0
            m_s2 = w4 * jnp.einsum('eci,ei->ec', ev, e1) * _inv(3)
            m_v1 = (w2 * es)[:, :, None] * e1[:, None, :]
            m_v2 = w3[:, :, None] * ev * e0[:, :, None]
            m_v3 = w5[:, :, None] * jnp.cross(ev, e1[:, None, :]) * _inv(2)
            mid_s = jnp.concatenate([m_s1, m_s2], axis=-1)
            mid_v = jnp.concatenate([m_v1, m_v2, m_v3], axis=1)
            inv_nn = 1.0 / jnp.sqrt(jnp.float32(NUM_NEIGHBORS))
            agg_s = jax.ops.segment_sum(mid_s, edge_dst, num_segments=n) * inv_nn
            agg_v = jax.ops.segment_sum(mid_v, edge_dst, num_segments=n) * inv_nn
            o_s = agg_s @ lin2_ws * a * _inv(S_MID)
            o_v = jnp.einsum('nci,cd->ndi', agg_v, lin2_wv) * a[:, :, None] * _inv(V_MID)
            pre_s = sc_s + o_s
            pre_v = sc_v + o_v
            scalars = jax.nn.silu(pre_s[:, :64])
            gates = jax.nn.sigmoid(pre_s[:, 64:96])
            gated = gates[:, :, None] * pre_v
            return jnp.concatenate([scalars, gated.reshape(n, 3 * V_OUT)], axis=-1)
        return _forward(node_features, node_attr, edge_attr, edge_scalars, lin1_ws, lin1_wv, fc_w1, fc_w2, sc_ws, sc_wv, lin2_ws, lin2_wv, edge_src, edge_dst)
    x = _layernorm(x + _L0_gnn_ref(x, node_vec1, src, dst, edge_attr_4, edge_attr_64, L0_gnn_lin1_ws, L0_gnn_lin1_wv, L0_gnn_fc_w1, L0_gnn_fc_w2, L0_gnn_sc_ws, L0_gnn_sc_wv, L0_gnn_lin2_ws, L0_gnn_lin2_wv), axis=-1)
    return x

_drawn_inputs = setup_inputs


def setup_inputs(seed=0):
    import zlib

    import numpy as np

    out = dict(_drawn_inputs(seed))
    spreads = {}
    factors = {}
    for name, (base, spread) in spreads.items():
        noise = np.random.default_rng([zlib.crc32(name.encode()), seed]).standard_normal(out[name].shape)
        drawn = base * np.exp(spread * noise) if base else spread * noise
        out[name] = jnp.asarray(drawn.astype(out[name].dtype))
    for name, factor in factors.items():
        out[name] = (out[name] * factor).astype(out[name].dtype)
    return out
```

```python
import math

import numpy as np

import concourse.bass as bass
from concourse import mybir
from concourse.alu_op_type import AluOpType as ALU

F32 = mybir.dt.float32
I32 = mybir.dt.int32
ACT = mybir.ActivationFunctionType
AX = mybir.AxisListType

P = 128
S_CH, V_CH = 64, 32
FEAT = S_CH + 3 * V_CH
HID = 64
W_COLS = 2 * S_CH + 3 * V_CH
O_S = 96
O_ALL = O_S + 3 * V_CH
COMP = 4
WINDOW = 32
PROD = 2 * S_CH + 9 * V_CH

TILES = 7
UNIT = TILES * P
STEPS = [(0, 1), (2, 3), (4, 5), (6,)]
GROUPS = [(ab, ts) for ts in STEPS for ab in (0, 1)]
NG = len(GROUPS)
ORDER = [(ab, t) for ab, ts in GROUPS for t in ts]
SLOTS = len(ORDER)
FIRST = [sum(len(ts) for _, ts in GROUPS[:g]) for g in range(NG)]
INDEX_COLS = [(FIRST[2 * q], FIRST[2 * q + 1] + len(STEPS[q])) for q in range(len(STEPS))]
HALF = FIRST[4]
HALF_COLS = 4 * P

C_W1 = 0
C_W2 = C_W1 + P
C_L1S = C_W2 + W_COLS
C_L1V = C_L1S + S_CH
C_SCS = C_L1V + 3 * V_CH
C_SCV = C_SCS + O_S
C_A = C_SCV + 3 * V_CH
C_V = C_A + P
C_C = C_V + 3 * O_ALL
W_PACK = C_C + V_CH

CROSS = [(0, 2, -1, 1), (1, 0, -1, 2), (1, 2, 1, 0), (2, 0, 1, 1), (0, 1, 1, 2), (2, 1, -1, 0)]


def build(nc, xs_d, xv_d, x_d, src_d, dst_tiles_d, dst_units_d, attr_d, edges_d, node_d, weights_d, out_d, n_nodes):
    node_tiles = math.ceil((n_nodes + 1) / P)
    NN = node_tiles * P
    n_units = dst_units_d.shape[0]
    pairs = n_units // 2
    last_base = NN - WINDOW
    last_rows = n_nodes - (node_tiles - 1) * P
    max_passes = math.ceil((n_nodes + 1) / WINDOW)
    assert n_nodes <= last_base and 0 < last_rows <= P

    sb = lambda name, shape, dt=F32: nc.alloc_sbuf_tensor(name, shape, dt)
    sem = nc.alloc_semaphore

    weights = sb("weights", [P, W_PACK])
    cross_neg = sb("cross_neg", [3 * V_CH, V_CH])
    node_attr = sb("node_attr", [P, node_tiles])
    attr = sb("attr", [P, pairs * SLOTS * COMP])
    rel = sb("rel", [P, pairs * SLOTS])
    dst_tiles = sb("dst_tiles", [P, pairs * SLOTS], I32)
    dst_units = sb("dst_units", [n_units, UNIT], I32)
    edges = sb("edges", [P, UNIT])
    index = [sb(f"index{q}", [P, b - a], I32) for q, (a, b) in enumerate(INDEX_COLS)]
    ident = sb("ident", [P, P])
    ones = sb("ones", [P, P])
    iota = sb("iota", [P, WINDOW])
    window_step = sb("window_step", [P, 1])
    sums_a = sb("sums_a", [P, 3 * NN])
    sums_v = sb("sums_v", [3 * V_CH, 6 * NN])
    lo = sb("lo", [n_units, 1])
    hi = sb("hi", [n_units, 1])
    span = sb("span", [n_units, 1], I32)
    span_windows = sb("span_windows", [n_units, 1], I32)
    passes = sb("passes", [n_units, 1])
    diag = sb("diag", [n_units, 2 * n_units])
    unit_rows = sb("unit_rows", [P, 2 * n_units])
    pair_passes = sb("pair_passes", [P, pairs])
    total = sb("total", [P, 1])
    base_i = sb("base_i", [P, n_units], I32)
    passes_i = sb("passes_i", [P, pairs + 1], I32)

    ARENA = 2 * NN + node_tiles * FEAT
    arena = sb("arena", [P, ARENA])
    xs = arena[0:S_CH, 0:NN]
    xv = arena[0:3 * V_CH, NN:2 * NN]
    h_all = arena[:, 2 * NN:].rearrange("p (i c) -> p i c", c=FEAT)
    at = [0]

    def cut(n):
        at[0] += n
        assert at[0] <= ARENA
        return arena[:, at[0] - n:at[0]]

    products = cut(4 * 2 * PROD).rearrange("p (g t c) -> p g t c", g=4, t=2)
    selector = cut(SLOTS * P)
    gathered = cut(SLOTS * FEAT).rearrange("p (j c) -> p j c", c=FEAT)
    sums_sb = cut(2 * PROD).rearrange("p (u c) -> p u c", u=2)
    hidden = cut(UNIT)
    onehot = cut(HALF * WINDOW)
    y_all = h_all
    small = sb("small", [P, 2 * O_S + 2 * FEAT + 2 * 6])
    gate_sb = small[:, 0:2 * O_S].rearrange("p (s c) -> p s c", s=2)
    stage_y = small[:, 2 * O_S:2 * O_S + 2 * FEAT].rearrange("p (s c) -> p s c", s=2)
    bn = small[:, 2 * O_S + 2 * FEAT:].rearrange("p (s c) -> p s c", s=2)
    moments = sb("moments", [P, node_tiles * 2])
    rstd = sb("rstd", [P, node_tiles])

    banks = [nc.alloc_psum_tensor(f"bank{i}", [P, 512], F32) for i in range(8)]
    w_ps = banks[0:4]
    sums_ps = banks[4:6]
    turned_ps = banks[6]
    hidden_ps = banks[7]
    turned = turned_ps[:, :]

    table = nc.dram_tensor("h_table", [NN, FEAT], F32, kind="Internal").ap()

    s_weights = sem("weights_loaded")
    s_nodes = sem("node_attr_loaded")
    s_x = [sem(f"x_loaded{i}") for i in range(2)]
    s_dstu = sem("dst_units_loaded")
    s_dstt = sem("dst_tiles_loaded")
    s_attr = sem("attr_loaded")
    s_const = sem("constants_made")
    s_const_step = sem("constant_steps")
    s_lin1 = sem("lin1_scaled")
    s_out_w = sem("output_weights_scaled")
    s_h_mm = sem("h_multiplied")
    s_h_sb = sem("h_scaled")
    s_table = sem("table_stored")
    s_diag = sem("unit_diagonals_made")
    s_rows = sem("unit_rows_multiplied")
    s_ctl = sem("loop_counts_ready")
    s_chain = sem("vector_step_done")
    s_rel = sem("window_moved")
    s_edges = sem("edges_loaded")
    s_index = [sem(f"index{q}_loaded") for q in range(len(INDEX_COLS))]
    s_gather = [sem(f"tile{j}_gathered") for j in range(SLOTS)]
    s_slot = sem("gather_slots_free")
    s_hid_mm = sem("hidden_multiplied")
    s_hid = sem("hidden_ready")
    s_w = sem("mlp_weights_ready")
    s_prod = sem("products_ready")
    s_onehot = sem("onehot_ready")
    s_sel = sem("selector_ready")
    s_agg = sem("group_summed")
    s_copied = [sem("sums_a_copied"), sem("sums_b_copied")]
    s_turned = sem("sums_transposed")
    s_added = sem("sums_added")
    s_zeroed = sem("accumulators_zeroed")
    s_xr = sem("x_rows_loaded")
    s_fin = sem("output_multiplied")
    s_gate = sem("gate_ready")
    s_yv = sem("residual_ready")
    s_mom = sem("moments_ready")
    s_std = sem("std_ready")
    s_norm = sem("rows_normalised")
    s_out = sem("output_stored")

    def w_of(rows, col, n):
        return weights[rows[0]:rows[1], col:col + n]

    def passes_of(eng, v):
        return eng.value_load(passes_i[0:1, bass.ds(v, 1)], min_val=1, max_val=max_passes)

    def counted(eng, reg):
        return eng.snap(reg, min_val=0, max_val=pairs * max_passes)

    X_SPLIT = (0, 13 * P, NN)

    with nc.Block() as block:

        @block.sync
        def _(sp):
            sp.dma_start(weights[:, :], weights_d).then_inc(s_weights, 16)
            sp.dma_start(dst_units[:, :], dst_units_d).then_inc(s_dstu, 16)
            for k in range(2):
                a, b = X_SPLIT[k:k + 2]
                sp.dma_start(xs[:, a:b], xs_d[:, a:b]).then_inc(s_x[k], 16)
                sp.dma_start(xv[:, a:b], xv_d[:, a:b]).then_inc(s_x[k], 16)
            sp.dma_start(attr[:, :], attr_d).then_inc(s_attr, 16)
            for a, b in ((0, 9), (9, 17), (17, node_tiles)):
                sp.wait_ge(s_h_sb, b)
                sp.dma_start(table[a * P:b * P, :].rearrange("(i p) c -> p i c", p=P),
                             h_all[:, a:b, :]).then_inc(s_table, 16)
            sp.wait_ge(s_ctl, 1)
            with sp.register("sync_iteration") as reg:
                sp.reg_mov(reg, 0)
                with sp.Fori(0, pairs) as v:
                    n = passes_of(sp, v)
                    with sp.Fori(0, n):
                        it = counted(sp, reg)
                        sp.wait_ge(s_hid_mm, it * 2 + 2)
                        sp.dma_start(edges[:, :], edges_d[bass.ds(v, 1), :, :].rearrange("a p n -> (a p) n"))\
                          .then_inc(s_edges, 16)
                        for q, (a, b) in enumerate(INDEX_COLS):
                            sp.wait_ge(s_prod, it * NG + 2 * (q + 1))
                            sp.dma_start(index[q][:, :],
                                         src_d[bass.ds(v, 1), :, a:b].rearrange("a p n -> (a p) n"))\
                              .then_inc(s_index[q], 16)
                        sp.reg_add(reg, reg, 1)
                it = counted(sp, reg)
                sp.wait_ge(s_hid_mm, it * 2 + 2)
                sp.dma_start(edges[:, :], edges_d[pairs - 1, :, :]).then_inc(s_edges, 16)
                sp.wait_ge(s_added, it * 2 + 4)
                sp.dma_start(xs, xs_d).then_inc(s_x[0], 16)
                sp.dma_start(xv, xv_d).then_inc(s_x[1], 16)
            full = node_tiles - 1
            sp.dma_start(y_all[:, 0:full, :], x_d[0:full * P, :].rearrange("(i p) c -> p i c", p=P))\
              .then_inc(s_xr, 16)
            sp.dma_start(y_all[0:last_rows, full, :], x_d[full * P:n_nodes, :]).then_inc(s_xr, 16)
            for a, b in ((0, 8), (8, 16), (16, full)):
                sp.wait_ge(s_norm, b)
                sp.dma_start(out_d[a * P:b * P, :].rearrange("(i p) c -> p i c", p=P), y_all[:, a:b, :])\
                  .then_inc(s_out, 16)
            sp.wait_ge(s_norm, node_tiles)
            sp.dma_start(out_d[full * P:n_nodes, :], y_all[0:last_rows, full, :]).then_inc(s_out, 16)
            sp.wait_ge(s_out, 4 * 16)

        @block.gpsimd
        def _(pool):
            pool.memset(ones[:, :], 1.0).then_inc(s_const, 1)
            pool.memset(ident[:, :], 0.0).then_inc(s_const_step, 1)
            pool.wait_ge(s_const_step, 1)
            pool.affine_select(out=ident[:, :], in_=ident[:, :], compare_op=ALU.not_equal, fill=1.0, base=0,
                               pattern=[[-1, P]], channel_multiplier=1).then_inc(s_const, 1)
            pool.iota(iota[:, :], pattern=[[1, WINDOW]], base=0, channel_multiplier=0,
                      allow_small_or_imprecise_dtypes=True).then_inc(s_const, 1)
            pool.memset(sums_v[:, :], 0.0).then_inc(s_zeroed, 1)
            pool.wait_ge(s_ctl, 1)
            with pool.register("pool_iteration") as reg:
                pool.reg_mov(reg, 0)
                with pool.Fori(0, pairs) as v:
                    n = passes_of(pool, v)
                    with pool.Fori(0, n):
                        it = counted(pool, reg)
                        for g, (ab, ts) in enumerate(GROUPS):
                            if g % 2 == 0:
                                pool.wait_ge(s_index[g // 2], it * 16 + 16)
                            pool.wait_ge(s_prod, it * NG + (g + 1))
                            pool.sem_inc(s_slot, 1)
                            for j in range(FIRST[g], FIRST[g] + len(ts)):
                                col = j - INDEX_COLS[g // 2][0]
                                pool.wait_ge(s_table, 3 * 16)
                                pool.indirect_dma_start(
                                    out=gathered[:, j, :], out_offset=None, in_=table,
                                    in_offset=bass.IndirectOffsetOnAxis(ap=index[g // 2][:, col:col + 1], axis=0))\
                                    .then_inc(s_gather[j], 16)
                        pool.reg_add(reg, reg, 1)

        @block.scalar
        def _(act):
            act.dma_start(node_attr[:, :], node_d).then_inc(s_nodes, 16)
            act.dma_start(dst_tiles[:, :], dst_tiles_d).then_inc(s_dstt, 16)
            act.wait_ge(s_nodes, 16)
            for i in range(node_tiles):
                act.wait_ge(s_h_mm, i + 1)
                nc.scalar.activation(h_all[:, i, :], w_ps[i % 4][:, 0:FEAT], ACT.Copy, scale=node_attr[:, i:i + 1])\
                  .then_inc(s_h_sb, 1)

            def silu(k, half, first):
                a, b = ((0, HALF_COLS), (HALF_COLS, UNIT))[half]
                act.wait_ge(s_hid_mm, k * 2 + (half + 3))
                if not first:
                    act.wait_ge(s_w, (k - 1) * NG + 4 * (half + 1))
                nc.scalar.activation(hidden[:, a:b], hidden_ps[:, 0:b - a], ACT.Silu, scale=1 / math.sqrt(HID))\
                  .then_inc(s_hid, 1)

            act.wait_ge(s_table, 3 * 16)
            silu(0, 0, True)
            silu(0, 1, True)
            act.wait_ge(s_ctl, 1)
            n_it = act.value_load(passes_i[0:1, pairs:pairs + 1], min_val=pairs, max_val=pairs * max_passes)
            with act.Fori(0, n_it) as it:
                silu(it + 1, 0, False)
                silu(it + 1, 1, False)
                for u in (0, 1):
                    act.wait_ge(s_agg, it * NG + (2 * NG - 1 + u))
                    act.wait_ge(s_turned, it * 2 + (u + 1))
                    nc.scalar.activation(sums_sb[:, u, :], sums_ps[u][:, 0:PROD], ACT.Copy)\
                      .then_inc(s_copied[u], 1)
            for i in range(node_tiles):
                rows = last_rows if i == node_tiles - 1 else P
                act.wait_ge(s_fin, i + 1)
                if i >= 2:
                    act.wait_ge(s_yv, i - 1)
                nc.scalar.activation(gate_sb[0:rows, i % 2, :], w_ps[i % 4][0:rows, 0:O_S], ACT.Sigmoid,
                                     scale=node_attr[0:rows, i:i + 1]).then_inc(s_gate, 1)
            act.wait_ge(s_mom, node_tiles + 1)
            nc.scalar.activation(rstd[:, :], rstd[:, :], ACT.Sqrt).then_inc(s_std, 1)

        @block.vector
        def _(dve):
            chain = [0]

            def link(ins):
                chain[0] += 1
                ins.then_inc(s_chain, 1)
                dve.wait_ge(s_chain, chain[0])

            def scale(rows, col, n, by):
                w = w_of(rows, col, n)
                return nc.vector.tensor_scalar(w, w, by, None, ALU.mult)

            dve.sem_inc(s_prod, NG)
            dve.sem_inc(s_added, 2)
            dve.wait_ge(s_weights, 16)
            scale((0, S_CH), C_L1S, S_CH, 1 / math.sqrt(S_CH))
            scale((0, 3 * V_CH), C_L1V, 3 * V_CH, 1 / math.sqrt(V_CH)).then_inc(s_lin1, 1)

            dve.wait_ge(s_dstu, 16)
            nc.vector.tensor_reduce(lo[:, :], dst_units[:, :], AX.X, ALU.min)
            link(nc.vector.tensor_reduce(hi[:, :], dst_units[:, :], AX.X, ALU.max))
            link(nc.vector.tensor_tensor(span[:, :], hi[:, :], lo[:, :], ALU.subtract))
            link(nc.vector.tensor_scalar(span_windows[:, :], span[:, :], int(math.log2(WINDOW)), None,
                                         ALU.logical_shift_right))
            link(nc.vector.tensor_scalar(passes[:, :], span_windows[:, :], 1.0, None, ALU.add))
            dve.wait_ge(s_const, 3)
            eye = ident[0:n_units, 0:n_units]
            nc.vector.tensor_scalar(diag[:, 0:n_units], eye, lo[:, 0:1], None, ALU.mult)
            nc.vector.tensor_scalar(diag[:, n_units:], eye, passes[:, 0:1], None, ALU.mult).then_inc(s_diag, 1)
            dve.wait_ge(s_rows, 1)
            link(nc.vector.tensor_copy(unit_rows[:, :], hidden_ps[:, 0:2 * n_units]))
            by_pair = unit_rows[:, n_units:].rearrange("p (v u) -> p v u", u=2)
            link(nc.vector.tensor_tensor(pair_passes[:, :], by_pair[:, :, 0], by_pair[:, :, 1], ALU.max))
            link(nc.vector.tensor_reduce(total[:, :], pair_passes[:, :], AX.X, ALU.add))
            nc.vector.tensor_copy(base_i[:, :], unit_rows[:, 0:n_units])
            nc.vector.tensor_copy(passes_i[:, 0:pairs], pair_passes[:, :])
            link(nc.vector.tensor_copy(passes_i[:, pairs:], total[:, :]))
            dve.sem_inc(s_ctl, 1)

            dve.wait_ge(s_dstt, 16)
            rel_v = rel[:, :].rearrange("p (v j) -> p v j", j=SLOTS)
            dst_v = dst_tiles[:, :].rearrange("p (v j) -> p v j", j=SLOTS)
            starts = unit_rows[:, 0:n_units].rearrange("p (v u) -> p v u", u=2)
            for u in (0, 1):
                quads = slice(0, 12)
                r = rel_v[:, :, quads].rearrange("p v (q u t) -> p v q u t", u=2, t=2)[:, :, :, u, :]
                d = dst_v[:, :, quads].rearrange("p v (q u t) -> p v q u t", u=2, t=2)[:, :, :, u, :]
                m = starts[:, :, u:u + 1].rearrange("p v (a b) -> p v a b", b=1).to_broadcast([P, pairs, 3, 2])
                nc.vector.tensor_tensor(r, d, m, ALU.subtract)
            link(nc.vector.tensor_tensor(rel_v[:, :, 12:14], dst_v[:, :, 12:14], starts, ALU.subtract))
            dve.sem_inc(s_rel, 1)

            c = 1 / math.sqrt(HID) / math.sqrt(16.0)
            scale((0, S_CH), C_SCS, O_S, 1 / math.sqrt(S_CH))
            scale((0, 3 * V_CH), C_SCV, 3 * V_CH, 1 / math.sqrt(V_CH))
            scale((0, S_CH), C_A, P, c / math.sqrt(96.0))
            scale((S_CH, P), C_A, P, c / math.sqrt(128.0))
            scale((0, V_CH), C_V, 3 * O_ALL, c / math.sqrt(128.0))
            scale((V_CH, 2 * V_CH), C_V, 3 * O_ALL, c / math.sqrt(96.0) / math.sqrt(3.0))
            rows = (2 * V_CH, 3 * V_CH)
            c3 = c / math.sqrt(128.0) / math.sqrt(2.0)
            for s in range(3):
                scale(rows, C_V + s * O_ALL, O_ALL, CROSS[s][2] * c3)
            nc.vector.tensor_scalar(cross_neg[:, :], w_of((0, 3 * V_CH), C_C, V_CH), -c3, None, ALU.mult)
            link(nc.vector.memset(window_step[:, :], float(WINDOW)))
            scale(rows, C_C, V_CH, c3).then_inc(s_out_w, 1)
            nc.vector.memset(sums_a[:, :], 0.0).then_inc(s_zeroed, 1)
            dve.wait_ge(s_table, 3 * 16)
            nc.vector.memset(sums_sb[:, 0, :], 0.0).then_inc(s_copied[0], 1)
            nc.vector.memset(sums_sb[:, 1, :], 0.0).then_inc(s_copied[1], 1)
            dve.wait_ge(s_attr, 16)
            dve.wait_ge(s_zeroed, 2)

            def multiply(it, g):
                ab, ts = GROUPS[g]
                n, j0 = len(ts), FIRST[g]
                w = w_ps[g % 4]
                dve.wait_ge(s_w, it * NG + (g + 1))
                dve.wait_ge(s_agg, it * NG + (g + 5))
                for k in range(n):
                    dve.wait_ge(s_gather[j0 + k], it * 16 + 16)
                wv = w[:, 0:n * W_COLS].rearrange("p (t c) -> p t c", t=n)
                es = gathered[:, j0:j0 + n, 0:S_CH].rearrange("p t (a c) -> p t a c", a=1)\
                    .to_broadcast([P, n, 2, S_CH])
                nc.vector.tensor_tensor(
                    products[:, g % 4, 0:n, 0:2 * S_CH].rearrange("p t (a c) -> p t a c", a=2),
                    wv[:, :, 0:2 * S_CH].rearrange("p t (a c) -> p t a c", a=2), es, ALU.mult)
                for k in range(n):
                    kinds = wv[:, k, 2 * S_CH:].rearrange("p (i a c) -> p i a c", i=1, a=3)\
                        .to_broadcast([P, 3, 3, V_CH])
                    ev = gathered[:, j0 + k, S_CH:].rearrange("p (i a c) -> p i a c", i=3, a=1)\
                        .to_broadcast([P, 3, 3, V_CH])
                    last = nc.vector.tensor_tensor(
                        products[:, g % 4, k, 2 * S_CH:].rearrange("p (i a c) -> p i a c", i=3, a=3),
                        kinds, ev, ALU.mult)
                last.then_inc(s_prod, 1)

            def select(it, v, half):
                a, b = ((0, HALF), (HALF, SLOTS))[half]
                n = b - a
                hot = onehot[:, 0:n * WINDOW].rearrange("p (j n) -> p j n", n=WINDOW)
                r = rel[:, bass.ds(v * SLOTS + a, n)].rearrange("p (j n) -> p j n", n=1).to_broadcast([P, n, WINDOW])
                io = iota[:, :].rearrange("p (j n) -> p j n", j=1).to_broadcast([P, n, WINDOW])
                dve.wait_ge(s_rel, it + 1)
                nc.vector.tensor_tensor(hot, io, r, ALU.is_equal).then_inc(s_onehot, 1)
                dve.wait_ge(s_onehot, it * 2 + (half + 1))
                dve.wait_ge(s_agg, it * NG + 4 * (half + 1))
                e = attr[:, bass.ds((v * SLOTS + a) * COMP, n * COMP)].rearrange("p (j k n) -> p j k n", k=COMP, n=1)\
                    .to_broadcast([P, n, COMP, WINDOW])
                nc.vector.tensor_tensor(
                    selector[:, a * P:b * P].rearrange("p (j k n) -> p j k n", k=COMP, n=WINDOW),
                    hot.rearrange("p j (k n) -> p j k n", k=1).to_broadcast([P, n, COMP, WINDOW]), e, ALU.mult)\
                    .then_inc(s_sel, 1)

            def add_sums(it, u, base):
                dve.wait_ge(s_turned, it * 2 + (u + 1))
                dve.wait_ge(s_added, it * 2 + (u + 2))

                def add(tensor, r0, r1, s0, n_sets, off, stride):
                    ps = bass.AP(turned_ps, r0 * 512 + off, [[512, r1 - r0], [stride, n_sets], [1, WINDOW]])
                    acc = tensor[r0:r1, s0 * NN:(s0 + n_sets) * NN].rearrange("p (s n) -> p s n", n=NN)\
                        [:, :, bass.ds(base, WINDOW)]
                    return nc.vector.tensor_tensor(acc, ps, acc, ALU.add)

                add(sums_a, 0, S_CH, 0, 1, 0, P)
                add(sums_a, S_CH, P, 0, 3, WINDOW, WINDOW)
                add(sums_v, 0, V_CH, 0, 3, P, P)
                add(sums_v, V_CH, 2 * V_CH, 0, 3, P + WINDOW, P + WINDOW)
                add(sums_v, 2 * V_CH, 3 * V_CH, 0, 4, P + 3 * WINDOW, 2 * WINDOW)
                add(sums_v, 2 * V_CH, 3 * V_CH, 4, 2, P + 2 * WINDOW, 2 * P).then_inc(s_added, 1)

            with dve.register("vector_iteration") as reg, dve.register("start_a") as reg_a, \
                    dve.register("start_b") as reg_b, dve.register("before_a") as old_a, \
                    dve.register("before_b") as old_b, dve.register("clamped") as tmp:
                dve.reg_mov(reg, 0)
                dve.reg_mov(old_a, 0)
                dve.reg_mov(old_b, 0)
                at_node = lambda r: dve.snap(r, min_val=0, max_val=last_base)
                with dve.Fori(0, pairs) as v:
                    n = passes_of(dve, v)
                    dve.reg_mov(reg_a, dve.value_load(base_i[0:1, bass.ds(v * 2, 1)], min_val=0, max_val=n_nodes))
                    dve.reg_mov(reg_b, dve.value_load(base_i[0:1, bass.ds(v * 2 + 1, 1)], min_val=0,
                                                      max_val=n_nodes))
                    with dve.Fori(0, n):
                        it = counted(dve, reg)
                        multiply(it, 0)
                        select(it, v, 0)
                        multiply(it, 1)
                        add_sums(it, 0, at_node(old_a))
                        multiply(it, 2)
                        multiply(it, 3)
                        select(it, v, 1)
                        r = rel[:, bass.ds(v * SLOTS, SLOTS)]
                        nc.vector.tensor_scalar(r, r, -float(WINDOW), None, ALU.add).then_inc(s_rel, 1)
                        multiply(it, 4)
                        add_sums(it, 1, at_node(old_b))
                        multiply(it, 5)
                        multiply(it, 6)
                        multiply(it, 7)
                        for start, old in ((reg_a, old_a), (reg_b, old_b)):
                            dve.reg_alu(old, start, last_base, ALU.min)
                            dve.reg_add(start, start, WINDOW)
                        dve.reg_add(reg, reg, 1)
                it = counted(dve, reg)
                add_sums(it, 0, at_node(old_a))
                add_sums(it, 1, at_node(old_b))

            dve.wait_ge(s_xr, 32)
            for i in range(node_tiles):
                rows = last_rows if i == node_tiles - 1 else P
                a = node_attr[0:rows, i:i + 1]
                o = w_ps[i % 4]
                gate = gate_sb[0:rows, i % 2, :]
                t = stage_y[0:rows, i % 2, :]
                dve.wait_ge(s_gate, i + 1)
                nc.vector.scalar_tensor_tensor(out=t[:, 0:S_CH], in0=o[0:rows, 0:S_CH], scalar=a,
                                               in1=gate[:, 0:S_CH], op0=ALU.mult, op1=ALU.mult)
                link(nc.vector.scalar_tensor_tensor(
                    out=t[:, S_CH:].rearrange("p (d k) -> p k d", k=3),
                    in0=o[0:rows, O_S:O_ALL].rearrange("p (k d) -> p k d", k=3), scalar=a,
                    in1=gate[:, S_CH:].rearrange("p (k d) -> p k d", k=1).to_broadcast([rows, 3, V_CH]),
                    op0=ALU.mult, op1=ALU.mult))
                y = y_all[0:rows, i, :]
                nc.vector.tensor_tensor(y, y, t, ALU.add).then_inc(s_yv, 1)
                dve.wait_ge(s_yv, i + 1)
                link(nc.vector.bn_stats(bn[0:rows, i % 2, :], y))
                nc.vector.bn_aggr(moments[0:rows, 2 * i:2 * i + 2], bn[0:rows, i % 2, :]).then_inc(s_mom, 1)
            dve.wait_ge(s_mom, node_tiles)
            full = node_tiles - 1
            variance = moments[:, :].rearrange("p (i m) -> p i m", m=2)[:, :, 1]
            link(nc.vector.memset(rstd[:, :], 1.0))
            nc.vector.tensor_scalar(rstd[:, 0:full], variance[:, 0:full], 1e-5, None, ALU.add)
            nc.vector.tensor_scalar(rstd[0:last_rows, full:], variance[0:last_rows, full:], 1e-5, None, ALU.add)\
              .then_inc(s_mom, 1)
            dve.wait_ge(s_std, 1)
            link(nc.vector.reciprocal(rstd[:, :], rstd[:, :]))
            for i in range(node_tiles):
                rows = last_rows if i == node_tiles - 1 else P
                y = y_all[0:rows, i, :]
                nc.vector.tensor_scalar(y, y, moments[0:rows, 2 * i:2 * i + 1], rstd[0:rows, i:i + 1],
                                        ALU.subtract, ALU.mult).then_inc(s_norm, 1)

        @block.tensor
        def _(pe):
            pe.sem_inc(s_agg, NG)
            pe.sem_inc(s_hid_mm, 2)
            pe.wait_ge(s_lin1, 1)
            for i in range(node_tiles):
                n0 = i * P
                if n0 in X_SPLIT:
                    pe.wait_ge(s_x[X_SPLIT.index(n0)], 32)
                if i >= 4:
                    pe.wait_ge(s_h_sb, i - 3)
                o = w_ps[i % 4]
                nc.tensor.matmul(o[:, 0:S_CH], xs[:, n0:n0 + P], w_of((0, S_CH), C_L1S, S_CH), start=True, stop=True)
                nc.tensor.matmul(o[:, S_CH:FEAT], xv[:, n0:n0 + P], w_of((0, 3 * V_CH), C_L1V, 3 * V_CH),
                                 start=True, stop=True).then_inc(s_h_mm, 1)
            pe.wait_ge(s_diag, 1)
            nc.tensor.matmul(hidden_ps[:, 0:2 * n_units], ones[0:n_units, :], diag[:, :], start=True, stop=True)\
              .then_inc(s_rows, 1)

            def hidden_half(k, half, first=False):
                a, b = ((0, HALF_COLS), (HALF_COLS, UNIT))[half]
                if half == 0:
                    pe.wait_ge(s_edges, k * 16 + 16)
                if half or not first:
                    pe.wait_ge(s_hid, k * 2 + half)
                nc.tensor.matmul(hidden_ps[:, 0:b - a], w_of((0, P), C_W1, P), edges[:, a:b], start=True, stop=True)\
                  .then_inc(s_hid_mm, 1)

            def mlp(it, g):
                ab, ts = GROUPS[g]
                r0 = ab * HID
                pe.wait_ge(s_hid, it * 2 + (1 + g // 4))
                pe.wait_ge(s_prod, it * NG + (g + 5))
                for k, t in enumerate(ts):
                    last = nc.tensor.matmul(w_ps[g % 4][:, k * W_COLS:(k + 1) * W_COLS],
                                            hidden[r0:r0 + HID, t * P:(t + 1) * P],
                                            w_of((r0, r0 + HID), C_W2, W_COLS), start=True, stop=True)
                last.then_inc(s_w, 1)

            def sum_group(it, g):
                ab, ts = GROUPS[g]
                if g % 4 == 0:
                    pe.wait_ge(s_sel, it * 2 + (1 + g // 4))
                if g < 2:
                    pe.wait_ge(s_copied[ab], it + 1)
                pe.wait_ge(s_prod, it * NG + (NG + g + 1))
                for k, t in enumerate(ts):
                    j = FIRST[g] + k
                    last = nc.tensor.matmul(sums_ps[ab][:, 0:PROD], selector[:, j * P:(j + 1) * P],
                                            products[:, g % 4, k, :], start=(t == 0), stop=(t == TILES - 1))
                last.then_inc(s_agg, 1)

            def turn(it, u):
                pe.wait_ge(s_copied[u], it + 1)
                pe.wait_ge(s_added, it * 2 + (u + 2))
                nc.tensor.transpose(turned[:, 0:P], sums_sb[:, u, 0:2 * S_CH], ident[:, :])
                for i in range(3):
                    c0 = 2 * S_CH + i * 3 * V_CH
                    last = nc.tensor.transpose(turned[0:3 * V_CH, (i + 1) * P:(i + 2) * P],
                                               sums_sb[:, u, c0:c0 + 3 * V_CH], ident[:, :])
                last.then_inc(s_turned, 1)

            pe.wait_ge(s_ctl, 1)
            hidden_half(0, 0, True)
            hidden_half(0, 1, True)
            mlp(0, 0)
            mlp(0, 1)
            n_it = pe.value_load(passes_i[0:1, pairs:pairs + 1], min_val=pairs, max_val=pairs * max_passes)
            with pe.Fori(0, n_it) as it:
                mlp(it, 2)
                mlp(it, 3)
                sum_group(it, 0)
                sum_group(it, 1)
                turn(it, 0)
                mlp(it, 4)
                mlp(it, 5)
                sum_group(it, 2)
                sum_group(it, 3)
                turn(it, 1)
                mlp(it, 6)
                mlp(it, 7)
                hidden_half(it + 1, 0)
                sum_group(it, 4)
                hidden_half(it + 1, 1)
                sum_group(it, 5)
                mlp(it + 1, 0)
                mlp(it + 1, 1)
                sum_group(it, 6)
                sum_group(it, 7)
            turn(n_it, 0)
            turn(n_it, 1)

            pe.wait_ge(s_added, n_it * 2 + 4)
            pe.wait_ge(s_out_w, 1)
            pe.wait_ge(s_x[0], 48)
            pe.wait_ge(s_x[1], 48)
            for i in range(node_tiles):
                if i >= 4:
                    pe.wait_ge(s_yv, i - 3)
                o = w_ps[i % 4]
                n0 = i * P
                terms = [(xs[:, n0:n0 + P], w_of((0, S_CH), C_SCS, O_S), 0),
                         (xv[:, n0:n0 + P], w_of((0, 3 * V_CH), C_SCV, 3 * V_CH), O_S),
                         (sums_a[:, n0:n0 + P], w_of((0, P), C_A, P), 0)]
                for s in (1, 2):
                    terms.append((sums_a[:, s * NN + n0:s * NN + n0 + P], w_of((0, P), C_A + O_S, V_CH),
                                  O_S + s * V_CH))
                for s in range(3):
                    terms.append((sums_v[:, s * NN + n0:s * NN + n0 + P],
                                  w_of((0, 3 * V_CH), C_V + s * O_ALL, O_ALL), 0))
                for s in range(3, 6):
                    _, _, sign, k = CROSS[s]
                    terms.append((sums_v[:, s * NN + n0:s * NN + n0 + P],
                                  w_of((0, 3 * V_CH), C_C, V_CH) if sign > 0 else cross_neg[:, :], O_S + k * V_CH))
                for n, (lhs, rhs, col) in enumerate(terms):
                    last = nc.tensor.matmul(o[:, col:col + rhs.shape[1]], lhs, rhs, start=(n == 0),
                                            stop=(n == len(terms) - 1), skip_group_check=True)
                last.then_inc(s_fin, 1)


def kernel(x, src, dst, edge_attr_4, edge_attr_64, node_vec1, L0_gnn_lin1_ws, L0_gnn_lin1_wv, L0_gnn_fc_w1,
           L0_gnn_fc_w2, L0_gnn_sc_ws, L0_gnn_sc_wv, L0_gnn_lin2_ws, L0_gnn_lin2_wv):
    import concourse.bacc as bacc
    from concourse.bass_utils import run_bass_kernel_spmd

    arr = lambda a: np.ascontiguousarray(a)
    x, src, dst, e4, e64, a = map(arr, (x, src, dst, edge_attr_4, edge_attr_64, node_vec1))
    w1, w2 = arr(L0_gnn_fc_w1), arr(L0_gnn_fc_w2)
    l1s, l1v, scs, scv = map(arr, (L0_gnn_lin1_ws, L0_gnn_lin1_wv, L0_gnn_sc_ws, L0_gnn_sc_wv))
    l2s, l2v = map(arr, (L0_gnn_lin2_ws, L0_gnn_lin2_wv))
    n, e = x.shape[0], src.shape[0]
    tiles = math.ceil((n + 1) / P)
    NN = tiles * P
    pairs = math.ceil(e / (2 * UNIT))
    e_pad = pairs * 2 * UNIT

    def padded(v, fill=0):
        out = np.full((e_pad,) + v.shape[1:], fill, v.dtype)
        out[:e] = v
        return out

    def by_tile(v):
        v = v.reshape((pairs, 2, TILES, P) + v.shape[1:])
        v = np.stack([v[:, ab, t] for ab, t in ORDER], axis=1)
        return np.ascontiguousarray(np.swapaxes(v, 1, 2))

    src_t = by_tile(padded(src))
    dst_p = padded(dst, n)
    dst_t = np.ascontiguousarray(by_tile(dst_p).transpose(1, 0, 2)).reshape(P, pairs * SLOTS)
    attr_t = np.ascontiguousarray(by_tile(padded(e4)).transpose(1, 0, 2, 3)).reshape(P, pairs * SLOTS * COMP)
    edges = np.ascontiguousarray(padded(e64).reshape(pairs, 2, UNIT, HID).transpose(0, 1, 3, 2))\
        .reshape(pairs, 2 * HID, UNIT)

    xs = np.zeros((S_CH, NN), x.dtype)
    xs[:, :n] = x[:, :S_CH].T
    xv = np.zeros((3 * V_CH, NN), x.dtype)
    xv[:, :n] = x[:, S_CH:].reshape(n, V_CH, 3).transpose(2, 1, 0).reshape(3 * V_CH, n)
    node = np.zeros((NN,), a.dtype)
    node[:n] = a[:, 0]
    node = np.ascontiguousarray(node.reshape(tiles, P).T)

    w = np.zeros((P, W_PACK), w1.dtype)
    for u in (0, 1):
        w[u * HID:(u + 1) * HID, C_W1 + u * HID:C_W1 + (u + 1) * HID] = w1
        w[u * HID:(u + 1) * HID, C_W2:C_W2 + W_COLS] = w2
    w[:S_CH, C_L1S:C_L1S + S_CH] = l1s
    w[:S_CH, C_SCS:C_SCS + O_S] = scs
    w[:S_CH, C_A:C_A + O_S] = l2s[:S_CH]
    w[S_CH:, C_A + O_S:C_A + P] = l2v[:S_CH]
    for i in range(3):
        rows = slice(i * V_CH, (i + 1) * V_CH)
        w[rows, C_L1V + i * V_CH:C_L1V + (i + 1) * V_CH] = l1v
        w[rows, C_SCV + i * V_CH:C_SCV + (i + 1) * V_CH] = scv
        c = C_V + i * O_ALL
        w[0:V_CH, c + O_S + i * V_CH:c + O_S + (i + 1) * V_CH] = l2v[S_CH:S_CH + V_CH]
        w[V_CH:2 * V_CH, c:c + O_S] = l2s[S_CH:]
        k = CROSS[i][3]
        w[2 * V_CH:3 * V_CH, c + O_S + k * V_CH:c + O_S + (k + 1) * V_CH] = l2v[S_CH + V_CH:]
    w[2 * V_CH:3 * V_CH, C_C:] = l2v[S_CH + V_CH:]

    arrays = {"xs": xs, "xv": xv, "x": x, "src": src_t, "dst_tiles": dst_t,
              "dst_units": dst_p.reshape(pairs * 2, UNIT), "attr": attr_t, "edges": edges, "node": node, "weights": w}
    nc = bacc.Bacc("TRN2", target_bir_lowering=False, num_devices=1)
    args = [nc.dram_tensor(f"{k}_dram", v.shape, mybir.dt.from_np(v.dtype), kind="ExternalInput").ap()
            for k, v in arrays.items()]
    out = nc.dram_tensor("out_dram", x.shape, F32, kind="ExternalOutput").ap()
    build(nc, *args, out, n)
    r = run_bass_kernel_spmd(nc, [{f"{k}_dram": v for k, v in arrays.items()}], core_ids=[0])
    return r.results[0]["out_dram"]
```

```python
import math

import numpy as np

import concourse.bass as bass
from concourse import mybir
from concourse.alu_op_type import AluOpType as ALU

F32 = mybir.dt.float32
F32R = mybir.dt.float32r
I32 = mybir.dt.int32
ACT = mybir.ActivationFunctionType
AX = mybir.AxisListType

P = 128
S_CH, V_CH = 64, 32
FEAT = S_CH + 3 * V_CH
HID = 64
W_COLS = 2 * S_CH + 3 * V_CH
O_S = 96
O_ALL = O_S + 3 * V_CH
COMP = 4
WINDOW = 32
PROD = 2 * S_CH + 9 * V_CH

TILES = 7
UNIT = TILES * P
STEPS = [(0, 1), (2, 3), (4, 5), (6,)]
GROUPS = [(ab, ts) for ts in STEPS for ab in (0, 1)]
NG = len(GROUPS)
ORDER = [(ab, t) for ab, ts in GROUPS for t in ts]
SLOTS = len(ORDER)
FIRST = [sum(len(ts) for _, ts in GROUPS[:g]) for g in range(NG)]
INDEX_COLS = [(FIRST[2 * q], FIRST[2 * q + 1] + len(STEPS[q])) for q in range(len(STEPS))]
HALF = FIRST[4]
HALF_COLS = 4 * P

C_W1 = 0
C_W2 = C_W1 + P
C_L1S = C_W2 + W_COLS
C_L1V = C_L1S + 3 * V_CH
C_A = C_L1V + 3 * V_CH
C_V = C_A + O_S
C_C = C_V + 3 * O_ALL
W_PACK = C_C + 3 * 3 * V_CH

CROSS = [(0, 2, -1, 1), (1, 0, -1, 2), (1, 2, 1, 0), (2, 0, 1, 1), (0, 1, 1, 2), (2, 1, -1, 0)]


def build(nc, xs_d, xv_d, x_d, src_d, dst_tiles_d, dst_units_d, attr_d, edges_d, node_d, weights_d, out_d, n_nodes):
    node_tiles = math.ceil((n_nodes + 1) / P)
    NN = node_tiles * P
    n_units = dst_units_d.shape[0]
    pairs = n_units // 2
    last_base = NN - WINDOW
    last_rows = n_nodes - (node_tiles - 1) * P
    max_passes = math.ceil((n_nodes + 1) / WINDOW)
    assert n_nodes <= last_base and 0 < last_rows <= P

    sb = lambda name, shape, dt=F32: nc.alloc_sbuf_tensor(name, shape, dt)
    sem = nc.alloc_semaphore

    weights = sb("weights", [P, W_PACK])
    node_attr = sb("node_attr", [P, node_tiles])
    attr = sb("attr", [P, pairs * SLOTS * COMP])
    rel = sb("rel", [P, pairs * SLOTS])
    dst_tiles = sb("dst_tiles", [P, pairs * SLOTS], I32)
    dst_units = sb("dst_units", [n_units, UNIT], I32)
    edges = sb("edges", [P, UNIT])
    index = [sb(f"index{q}", [P, b - a], I32) for q, (a, b) in enumerate(INDEX_COLS)]
    ident = sb("ident", [P, P])
    ones = sb("ones", [P, P])
    iota = sb("iota", [P, WINDOW])
    sums_1 = sb("sums_1", [P, NN])
    sums_v = sb("sums_v", [P, 6 * NN])
    lo = sb("lo", [n_units, 1])
    hi = sb("hi", [n_units, 1])
    span = sb("span", [n_units, 1], I32)
    span_windows = sb("span_windows", [n_units, 1], I32)
    passes = sb("passes", [n_units, 1])
    diag = sb("diag", [n_units, 2 * n_units])
    unit_rows = sb("unit_rows", [P, 2 * n_units])
    pair_passes = sb("pair_passes", [P, pairs])
    total = sb("total", [P, 1])
    base_i = sb("base_i", [P, n_units], I32)
    passes_i = sb("passes_i", [P, pairs + 1], I32)

    ARENA = 2 * NN + node_tiles * FEAT
    arena = sb("arena", [P, ARENA])
    xs = arena[0:S_CH, 0:NN]
    xv = arena[0:3 * V_CH, NN:2 * NN]
    h_all = arena[:, 2 * NN:].rearrange("p (i c) -> p i c", c=FEAT)
    at = [0]

    def cut(n):
        at[0] += n
        assert at[0] <= ARENA
        return arena[:, at[0] - n:at[0]]

    products = cut(NG * 2 * PROD).rearrange("p (g t c) -> p g t c", g=NG, t=2)
    gathered = cut(SLOTS * FEAT).rearrange("p (j c) -> p j c", c=FEAT)
    sums_sb = cut(2 * PROD).rearrange("p (u c) -> p u c", u=2)
    onehot = cut(SLOTS * WINDOW)
    y_all = h_all
    selector = sb("selector", [P, SLOTS * P])
    hidden = sb("hidden", [P, UNIT])
    hidden_parts = sb("hidden_parts", [P, 2 * UNIT], F32R)
    w2_high = sb("w2_high", [P, W_COLS], F32R)
    w2_low = sb("w2_low", [P, W_COLS], F32R)
    small = sb("small", [P, 2 * O_S + 2 * FEAT + 2 * 6])
    gate_sb = small[:, 0:2 * O_S].rearrange("p (s c) -> p s c", s=2)
    stage_y = small[:, 2 * O_S:2 * O_S + 2 * FEAT].rearrange("p (s c) -> p s c", s=2)
    bn = small[:, 2 * O_S + 2 * FEAT:].rearrange("p (s c) -> p s c", s=2)
    moments = sb("moments", [P, node_tiles * 2])
    rstd = sb("rstd", [P, node_tiles])

    banks = [nc.alloc_psum_tensor(f"bank{i}", [P, 512], F32) for i in range(8)]
    w_ps = banks[0:4]
    sums_ps = banks[4:6]
    turned_ps = banks[6]
    hidden_ps = banks[7]
    turned = turned_ps[:, :]

    table = nc.dram_tensor("h_table", [NN, FEAT], F32, kind="Internal").ap()

    s_weights = sem("weights_loaded")
    s_nodes = sem("node_attr_loaded")
    s_x = [sem(f"x_loaded{i}") for i in range(2)]
    s_dstu = sem("dst_units_loaded")
    s_dstt = sem("dst_tiles_loaded")
    s_attr = sem("attr_loaded")
    s_const = sem("constants_made")
    s_const_step = sem("constant_steps")
    s_lin1 = sem("lin1_scaled")
    s_out_w = sem("output_weights_scaled")
    s_h_mm = sem("h_multiplied")
    s_h_sb = sem("h_scaled")
    s_table = sem("table_stored")
    s_diag = sem("unit_diagonals_made")
    s_rows = sem("unit_rows_multiplied")
    s_ctl = sem("loop_counts_ready")
    s_chain = sem("vector_step_done")
    s_rel = sem("window_moved")
    s_edges = sem("edges_loaded")
    s_index = [sem(f"index{q}_loaded") for q in range(len(INDEX_COLS))]
    s_gather = [sem(f"tile{j}_gathered") for j in range(SLOTS)]
    s_slot = sem("gather_slots_free")
    s_hid_mm = sem("hidden_multiplied")
    s_hid = sem("hidden_high_part_ready")
    s_split = sem("hidden_low_part_ready")
    s_w2 = sem("w2_split")
    s_w = sem("mlp_weights_ready")
    s_prod = sem("products_ready")
    s_onehot = sem("onehot_ready")
    s_sel = sem("selector_ready")
    s_agg = sem("group_summed")
    s_copied = [sem("sums_a_copied"), sem("sums_b_copied")]
    s_turned = sem("sums_transposed")
    s_added = sem("sums_added")
    s_zeroed = sem("accumulators_zeroed")
    s_xsum = sem("x_placed_in_accumulators")
    s_xr = sem("x_rows_loaded")
    s_fin = sem("output_multiplied")
    s_gate = sem("gate_ready")
    s_yv = sem("residual_ready")
    s_mom = sem("moments_ready")
    s_std = sem("std_ready")
    s_norm = sem("rows_normalised")
    s_out = sem("output_stored")

    def w_of(rows, col, n):
        return weights[rows[0]:rows[1], col:col + n]

    def passes_of(eng, v):
        return eng.value_load(passes_i[0:1, bass.ds(v, 1)], min_val=1, max_val=max_passes)

    def counted(eng, reg):
        return eng.snap(reg, min_val=0, max_val=pairs * max_passes)

    X_SPLIT = (0, 13 * P, NN)

    with nc.Block() as block:

        @block.sync
        def _(sp):
            sp.dma_start(weights[:, :], weights_d).then_inc(s_weights, 16)
            sp.dma_start(dst_units[:, :], dst_units_d).then_inc(s_dstu, 16)
            for k in range(2):
                a, b = X_SPLIT[k:k + 2]
                sp.dma_start(xs[:, a:b], xs_d[:, a:b]).then_inc(s_x[k], 16)
                sp.dma_start(xv[:, a:b], xv_d[:, a:b]).then_inc(s_x[k], 16)
            sp.dma_start(attr[:, :], attr_d).then_inc(s_attr, 16)
            for a, b in ((0, 9), (9, 17), (17, node_tiles)):
                sp.wait_ge(s_h_sb, b)
                sp.dma_start(table[a * P:b * P, :].rearrange("(i p) c -> p i c", p=P),
                             h_all[:, a:b, :]).then_inc(s_table, 16)
            sp.wait_ge(s_ctl, 1)
            with sp.register("sync_iteration") as reg:
                sp.reg_mov(reg, 0)
                with sp.Fori(0, pairs) as v:
                    n = passes_of(sp, v)
                    with sp.Fori(0, n):
                        it = counted(sp, reg)
                        sp.wait_ge(s_hid_mm, it * 2 + 2)
                        sp.dma_start(edges[:, :], edges_d[bass.ds(v, 1), :, :].rearrange("a p n -> (a p) n"))\
                          .then_inc(s_edges, 16)
                        for q, (a, b) in enumerate(INDEX_COLS):
                            sp.wait_ge(s_prod, it * NG + 2 * (q + 1))
                            sp.dma_start(index[q][:, :],
                                         src_d[bass.ds(v, 1), :, a:b].rearrange("a p n -> (a p) n"))\
                              .then_inc(s_index[q], 16)
                        sp.reg_add(reg, reg, 1)
                it = counted(sp, reg)
                sp.wait_ge(s_hid_mm, it * 2 + 2)
                sp.dma_start(edges[:, :], edges_d[pairs - 1, :, :]).then_inc(s_edges, 16)
                sp.wait_ge(s_added, it * 2 + 4)
            full = node_tiles - 1
            sp.dma_start(y_all[:, 0:full, :], x_d[0:full * P, :].rearrange("(i p) c -> p i c", p=P))\
              .then_inc(s_xr, 16)
            sp.dma_start(y_all[0:last_rows, full, :], x_d[full * P:n_nodes, :]).then_inc(s_xr, 16)
            for a, b in ((0, 8), (8, 16), (16, full)):
                sp.wait_ge(s_norm, b)
                sp.dma_start(out_d[a * P:b * P, :].rearrange("(i p) c -> p i c", p=P), y_all[:, a:b, :])\
                  .then_inc(s_out, 16)
            sp.wait_ge(s_norm, node_tiles)
            sp.dma_start(out_d[full * P:n_nodes, :], y_all[0:last_rows, full, :]).then_inc(s_out, 16)
            sp.wait_ge(s_out, 4 * 16)

        @block.gpsimd
        def _(pool):
            pool.memset(ones[:, :], 1.0).then_inc(s_const, 1)
            pool.memset(ident[:, :], 0.0).then_inc(s_const_step, 1)
            pool.wait_ge(s_const_step, 1)
            pool.affine_select(out=ident[:, :], in_=ident[:, :], compare_op=ALU.not_equal, fill=1.0, base=0,
                               pattern=[[-1, P]], channel_multiplier=1).then_inc(s_const, 1)
            pool.iota(iota[:, :], pattern=[[1, WINDOW]], base=0, channel_multiplier=0,
                      allow_small_or_imprecise_dtypes=True).then_inc(s_const, 1)
            pool.memset(sums_v[0:3 * V_CH, :], 0.0).then_inc(s_zeroed, 1)
            pool.wait_ge(s_ctl, 1)
            with pool.register("pool_iteration") as reg:
                pool.reg_mov(reg, 0)
                with pool.Fori(0, pairs) as v:
                    n = passes_of(pool, v)
                    with pool.Fori(0, n):
                        it = counted(pool, reg)
                        for g, (ab, ts) in enumerate(GROUPS):
                            if g % 2 == 0:
                                pool.wait_ge(s_index[g // 2], it * 16 + 16)
                            pool.wait_ge(s_prod, it * NG + (g + 1))
                            pool.sem_inc(s_slot, 1)
                            for j in range(FIRST[g], FIRST[g] + len(ts)):
                                col = j - INDEX_COLS[g // 2][0]
                                pool.wait_ge(s_table, 3 * 16)
                                pool.indirect_dma_start(
                                    out=gathered[:, j, :], out_offset=None, in_=table,
                                    in_offset=bass.IndirectOffsetOnAxis(ap=index[g // 2][:, col:col + 1], axis=0))\
                                    .then_inc(s_gather[j], 16)
                        pool.reg_add(reg, reg, 1)

        @block.scalar
        def _(act):
            act.dma_start(node_attr[:, :], node_d).then_inc(s_nodes, 16)
            act.dma_start(dst_tiles[:, :], dst_tiles_d).then_inc(s_dstt, 16)
            act.wait_ge(s_nodes, 16)
            for i in range(node_tiles):
                act.wait_ge(s_h_mm, i + 1)
                nc.scalar.activation(h_all[:, i, :], w_ps[i % 4][:, 0:FEAT], ACT.Copy, scale=node_attr[:, i:i + 1])\
                  .then_inc(s_h_sb, 1)

            act.dma_start(sums_1[S_CH:P, :], xs_d).then_inc(s_xsum, 16)
            for i in range(3):
                act.dma_start(sums_v[3 * V_CH:P, 2 * i * NN:(2 * i + 1) * NN], xv_d[i * V_CH:(i + 1) * V_CH, :])\
                   .then_inc(s_xsum, 16)

            def silu(k, half, first):
                a, b = ((0, HALF_COLS), (HALF_COLS, UNIT))[half]
                act.wait_ge(s_hid_mm, k * 2 + (half + 3))
                if not first:
                    act.wait_ge(s_w, (k - 1) * NG + 4 * (half + 1))
                    act.wait_ge(s_split, (k - 1) * 2 + (half + 1))
                nc.scalar.activation(hidden[:, a:b], hidden_ps[:, 0:b - a], ACT.Silu, scale=1 / math.sqrt(HID))
                for u in (0, 1):
                    r = slice(u * HID, (u + 1) * HID)
                    last = nc.scalar.activation(hidden_parts[r, u * UNIT + a:u * UNIT + b], hidden_ps[r, 0:b - a],
                                                ACT.Silu, scale=1 / math.sqrt(HID))
                last.then_inc(s_hid, 1)

            silu(0, 0, True)
            silu(0, 1, True)
            act.wait_ge(s_ctl, 1)
            n_it = act.value_load(passes_i[0:1, pairs:pairs + 1], min_val=pairs, max_val=pairs * max_passes)
            with act.Fori(0, n_it) as it:
                silu(it + 1, 0, False)
                silu(it + 1, 1, False)
                for u in (0, 1):
                    act.wait_ge(s_agg, it * NG + (2 * NG - 1 + u))
                    act.wait_ge(s_turned, it * 2 + (u + 1))
                    nc.scalar.activation(sums_sb[:, u, :], sums_ps[u][:, 0:PROD], ACT.Copy)\
                      .then_inc(s_copied[u], 1)
            for i in range(node_tiles):
                rows = last_rows if i == node_tiles - 1 else P
                act.wait_ge(s_fin, i + 1)
                if i >= 2:
                    act.wait_ge(s_yv, i - 1)
                nc.scalar.activation(gate_sb[0:rows, i % 2, :], w_ps[i % 4][0:rows, 0:O_S], ACT.Sigmoid,
                                     scale=node_attr[0:rows, i:i + 1]).then_inc(s_gate, 1)
            act.wait_ge(s_mom, node_tiles + 1)
            nc.scalar.activation(rstd[:, :], rstd[:, :], ACT.Sqrt).then_inc(s_std, 1)

        @block.vector
        def _(dve):
            chain = [0]

            def link(ins):
                chain[0] += 1
                ins.then_inc(s_chain, 1)
                dve.wait_ge(s_chain, chain[0])

            def scale(rows, col, n, by):
                w = w_of(rows, col, n)
                return nc.vector.tensor_scalar(w, w, by, None, ALU.mult)

            dve.sem_inc(s_prod, NG)
            dve.sem_inc(s_added, 2)
            dve.wait_ge(s_weights, 16)
            scale((0, S_CH), C_L1S, S_CH, 1 / math.sqrt(S_CH))
            scale((0, 3 * V_CH), C_L1V, 3 * V_CH, 1 / math.sqrt(V_CH)).then_inc(s_lin1, 1)

            w2 = w_of((0, P), C_W2, W_COLS)
            link(nc.vector.tensor_copy(w2_high[:, :], w2))
            nc.vector.tensor_tensor(w2_low[:, :], w2, w2_high[:, :].bitcast(F32), ALU.subtract).then_inc(s_w2, 1)

            dve.wait_ge(s_dstu, 16)
            nc.vector.tensor_reduce(lo[:, :], dst_units[:, :], AX.X, ALU.min)
            link(nc.vector.tensor_reduce(hi[:, :], dst_units[:, :], AX.X, ALU.max))
            link(nc.vector.tensor_tensor(span[:, :], hi[:, :], lo[:, :], ALU.subtract))
            link(nc.vector.tensor_scalar(span_windows[:, :], span[:, :], int(math.log2(WINDOW)), None,
                                         ALU.logical_shift_right))
            link(nc.vector.tensor_scalar(passes[:, :], span_windows[:, :], 1.0, None, ALU.add))
            dve.wait_ge(s_const, 3)
            eye = ident[0:n_units, 0:n_units]
            nc.vector.tensor_scalar(diag[:, 0:n_units], eye, lo[:, 0:1], None, ALU.mult)
            nc.vector.tensor_scalar(diag[:, n_units:], eye, passes[:, 0:1], None, ALU.mult).then_inc(s_diag, 1)
            dve.wait_ge(s_rows, 1)
            link(nc.vector.tensor_copy(unit_rows[:, :], hidden_ps[:, 0:2 * n_units]))
            by_pair = unit_rows[:, n_units:].rearrange("p (v u) -> p v u", u=2)
            link(nc.vector.tensor_tensor(pair_passes[:, :], by_pair[:, :, 0], by_pair[:, :, 1], ALU.max))
            link(nc.vector.tensor_reduce(total[:, :], pair_passes[:, :], AX.X, ALU.add))
            nc.vector.tensor_copy(base_i[:, :], unit_rows[:, 0:n_units])
            nc.vector.tensor_copy(passes_i[:, 0:pairs], pair_passes[:, :])
            link(nc.vector.tensor_copy(passes_i[:, pairs:], total[:, :]))
            dve.sem_inc(s_ctl, 1)

            dve.wait_ge(s_dstt, 16)
            rel_v = rel[:, :].rearrange("p (v j) -> p v j", j=SLOTS)
            dst_v = dst_tiles[:, :].rearrange("p (v j) -> p v j", j=SLOTS)
            starts = unit_rows[:, 0:n_units].rearrange("p (v u) -> p v u", u=2)
            for u in (0, 1):
                quads = slice(0, 12)
                r = rel_v[:, :, quads].rearrange("p v (q u t) -> p v q u t", u=2, t=2)[:, :, :, u, :]
                d = dst_v[:, :, quads].rearrange("p v (q u t) -> p v q u t", u=2, t=2)[:, :, :, u, :]
                m = starts[:, :, u:u + 1].rearrange("p v (a b) -> p v a b", b=1).to_broadcast([P, pairs, 3, 2])
                nc.vector.tensor_tensor(r, d, m, ALU.subtract)
            link(nc.vector.tensor_tensor(rel_v[:, :, 12:14], dst_v[:, :, 12:14], starts, ALU.subtract))
            dve.sem_inc(s_rel, 1)

            c = 1 / math.sqrt(HID) / math.sqrt(16.0)
            scale((0, S_CH), C_A, O_S, c / math.sqrt(96.0))
            scale((S_CH, P), C_A, O_S, 1 / math.sqrt(S_CH))
            scale((0, V_CH), C_V, 3 * O_ALL, c / math.sqrt(128.0))
            scale((V_CH, 2 * V_CH), C_V, 3 * O_ALL, c / math.sqrt(96.0) / math.sqrt(3.0))
            scale((3 * V_CH, P), C_V, 3 * O_ALL, 1 / math.sqrt(V_CH))
            scale((0, 2 * V_CH), C_C, 9 * V_CH, c / math.sqrt(128.0))
            rows = (2 * V_CH, 3 * V_CH)
            c3 = c / math.sqrt(128.0) / math.sqrt(2.0)
            for i in range(3):
                scale(rows, C_V + i * O_ALL, O_ALL, CROSS[2 * i][2] * c3)
            for k in range(3):
                last = scale(rows, C_C + k * 3 * V_CH, 3 * V_CH, CROSS[5 - 2 * k][2] * c3)
            last.then_inc(s_out_w, 1)
            nc.vector.memset(sums_1[0:S_CH, :], 0.0).then_inc(s_zeroed, 1)
            dve.wait_ge(s_table, 3 * 16)
            nc.vector.memset(sums_sb[:, 0, :], 0.0).then_inc(s_copied[0], 1)
            nc.vector.memset(sums_sb[:, 1, :], 0.0).then_inc(s_copied[1], 1)
            dve.wait_ge(s_attr, 16)
            dve.wait_ge(s_zeroed, 2)

            def multiply(it, g):
                ab, ts = GROUPS[g]
                n, j0 = len(ts), FIRST[g]
                w = w_ps[g % 4]
                dve.wait_ge(s_w, it * NG + (g + 1))
                dve.wait_ge(s_agg, it * NG + (g + 1))
                for k in range(n):
                    dve.wait_ge(s_gather[j0 + k], it * 16 + 16)
                wv = w[:, 0:n * W_COLS].rearrange("p (t c) -> p t c", t=n)
                es = gathered[:, j0:j0 + n, 0:S_CH].rearrange("p t (a c) -> p t a c", a=1)\
                    .to_broadcast([P, n, 2, S_CH])
                nc.vector.tensor_tensor(
                    products[:, g, 0:n, 0:2 * S_CH].rearrange("p t (a c) -> p t a c", a=2),
                    wv[:, :, 0:2 * S_CH].rearrange("p t (a c) -> p t a c", a=2), es, ALU.mult)
                for k in range(n):
                    kinds = wv[:, k, 2 * S_CH:].rearrange("p (i a c) -> p i a c", i=1, a=3)\
                        .to_broadcast([P, 3, 3, V_CH])
                    ev = gathered[:, j0 + k, S_CH:].rearrange("p (i a c) -> p i a c", i=3, a=1)\
                        .to_broadcast([P, 3, 3, V_CH])
                    last = nc.vector.tensor_tensor(
                        products[:, g, k, 2 * S_CH:].rearrange("p (i a c) -> p i a c", i=3, a=3),
                        kinds, ev, ALU.mult)
                last.then_inc(s_prod, 1)

            def split(k, half):
                a, b = ((0, HALF_COLS), (HALF_COLS, UNIT))[half]
                dve.wait_ge(s_hid, k * 2 + (half + 1))
                for u in (0, 1):
                    own, other = (slice(x * HID, (x + 1) * HID) for x in (u, 1 - u))
                    last = nc.vector.tensor_tensor(
                        hidden_parts[other, u * UNIT + a:u * UNIT + b], hidden[own, a:b],
                        hidden_parts[own, u * UNIT + a:u * UNIT + b].bitcast(F32), ALU.subtract)
                last.then_inc(s_split, 1)

            def hot_of(half):
                n = (HALF, SLOTS - HALF)[half]
                return n, onehot[:, half * HALF * WINDOW:(half * HALF + n) * WINDOW].rearrange("p (j n) -> p j n", n=WINDOW)

            def point(it, v, half):
                n, hot = hot_of(half)
                r = rel[:, bass.ds(v * SLOTS + half * HALF, n)].rearrange("p (j n) -> p j n", n=1)\
                    .to_broadcast([P, n, WINDOW])
                io = iota[:, :].rearrange("p (j n) -> p j n", j=1).to_broadcast([P, n, WINDOW])
                dve.wait_ge(s_rel, it + 1)
                nc.vector.tensor_tensor(hot, io, r, ALU.is_equal).then_inc(s_onehot, 1)

            def select(it, v, half):
                n, hot = hot_of(half)
                a = half * HALF
                dve.wait_ge(s_onehot, it * 2 + (half + 1))
                dve.wait_ge(s_agg, it * NG + 4 * (half + 1))
                e = attr[:, bass.ds((v * SLOTS + a) * COMP, n * COMP)].rearrange("p (j k n) -> p j k n", k=COMP, n=1)\
                    .to_broadcast([P, n, COMP, WINDOW])
                nc.vector.tensor_tensor(
                    selector[:, a * P:(a + n) * P].rearrange("p (j k n) -> p j k n", k=COMP, n=WINDOW),
                    hot.rearrange("p j (k n) -> p j k n", k=1).to_broadcast([P, n, COMP, WINDOW]), e, ALU.mult)\
                    .then_inc(s_sel, 1)

            def add_sums(it, u, base):
                dve.wait_ge(s_turned, it * 2 + (u + 1))
                dve.wait_ge(s_added, it * 2 + (u + 2))

                def add(tensor, r0, src0, rows, set0, set_step, n_sets, off, stride):
                    ps = bass.AP(turned_ps, src0 * 512 + off, [[512, rows], [stride, n_sets], [1, WINDOW]])
                    acc = tensor[r0:r0 + rows, :].rearrange("p (s n) -> p s n", n=NN)\
                        [:, set0:set0 + set_step * (n_sets - 1) + 1:set_step, bass.ds(base, WINDOW)]
                    return nc.vector.tensor_tensor(acc, ps, acc, ALU.add)

                k0 = WINDOW
                add(sums_1, 0, 0, S_CH, 0, 1, 1, 0, P)
                add(sums_v, 0, S_CH, S_CH, 1, 2, 3, k0 + 2 * WINDOW, -WINDOW)
                add(sums_v, 0, 0, V_CH, 0, 2, 3, P, P)
                add(sums_v, V_CH, V_CH, V_CH, 0, 2, 3, P + k0, P + WINDOW)
                add(sums_v, 2 * V_CH, 2 * V_CH, V_CH, 0, 1, 4, P + k0 + 2 * WINDOW, 2 * WINDOW)
                add(sums_v, 2 * V_CH, 2 * V_CH, V_CH, 4, 1, 2, P + k0 + WINDOW, 2 * P).then_inc(s_added, 1)

            split(0, 0)
            with dve.register("vector_iteration") as reg, dve.register("start_a") as reg_a, \
                    dve.register("start_b") as reg_b, dve.register("before_a") as old_a, \
                    dve.register("before_b") as old_b, dve.register("clamped") as tmp:
                dve.reg_mov(reg, 0)
                dve.reg_mov(old_a, 0)
                dve.reg_mov(old_b, 0)
                at_node = lambda r: dve.snap(r, min_val=0, max_val=last_base)
                with dve.Fori(0, pairs) as v:
                    n = passes_of(dve, v)
                    dve.reg_mov(reg_a, dve.value_load(base_i[0:1, bass.ds(v * 2, 1)], min_val=0, max_val=n_nodes))
                    dve.reg_mov(reg_b, dve.value_load(base_i[0:1, bass.ds(v * 2 + 1, 1)], min_val=0,
                                                      max_val=n_nodes))
                    with dve.Fori(0, n):
                        it = counted(dve, reg)
                        point(it, v, 0)
                        multiply(it, 0)
                        select(it, v, 0)
                        split(it, 1)
                        point(it, v, 1)
                        multiply(it, 1)
                        multiply(it, 2)
                        multiply(it, 3)
                        add_sums(it, 0, at_node(old_a))
                        multiply(it, 4)
                        split(it + 1, 0)
                        select(it, v, 1)
                        multiply(it, 5)
                        r = rel[:, bass.ds(v * SLOTS, SLOTS)]
                        nc.vector.tensor_scalar(r, r, -float(WINDOW), None, ALU.add).then_inc(s_rel, 1)
                        multiply(it, 6)
                        multiply(it, 7)
                        add_sums(it, 1, at_node(old_b))
                        for start, old in ((reg_a, old_a), (reg_b, old_b)):
                            dve.reg_alu(old, start, last_base, ALU.min)
                            dve.reg_add(start, start, WINDOW)
                        dve.reg_add(reg, reg, 1)
                it = counted(dve, reg)
                add_sums(it, 0, at_node(old_a))
                add_sums(it, 1, at_node(old_b))

            dve.wait_ge(s_xr, 32)
            for i in range(node_tiles):
                rows = last_rows if i == node_tiles - 1 else P
                a = node_attr[0:rows, i:i + 1]
                o = w_ps[i % 4]
                gate = gate_sb[0:rows, i % 2, :]
                t = stage_y[0:rows, i % 2, :]
                dve.wait_ge(s_gate, i + 1)
                nc.vector.scalar_tensor_tensor(out=t[:, 0:S_CH], in0=o[0:rows, 0:S_CH], scalar=a,
                                               in1=gate[:, 0:S_CH], op0=ALU.mult, op1=ALU.mult)
                link(nc.vector.scalar_tensor_tensor(
                    out=t[:, S_CH:].rearrange("p (d k) -> p k d", k=3),
                    in0=o[0:rows, O_S:O_ALL].rearrange("p (k d) -> p k d", k=3), scalar=a,
                    in1=gate[:, S_CH:].rearrange("p (k d) -> p k d", k=1).to_broadcast([rows, 3, V_CH]),
                    op0=ALU.mult, op1=ALU.mult))
                y = y_all[0:rows, i, :]
                nc.vector.tensor_tensor(y, y, t, ALU.add).then_inc(s_yv, 1)
                dve.wait_ge(s_yv, i + 1)
                link(nc.vector.bn_stats(bn[0:rows, i % 2, :], y))
                nc.vector.bn_aggr(moments[0:rows, 2 * i:2 * i + 2], bn[0:rows, i % 2, :]).then_inc(s_mom, 1)
            dve.wait_ge(s_mom, node_tiles)
            full = node_tiles - 1
            variance = moments[:, :].rearrange("p (i m) -> p i m", m=2)[:, :, 1]
            link(nc.vector.memset(rstd[:, :], 1.0))
            nc.vector.tensor_scalar(rstd[:, 0:full], variance[:, 0:full], 1e-5, None, ALU.add)
            nc.vector.tensor_scalar(rstd[0:last_rows, full:], variance[0:last_rows, full:], 1e-5, None, ALU.add)\
              .then_inc(s_mom, 1)
            dve.wait_ge(s_std, 1)
            link(nc.vector.reciprocal(rstd[:, :], rstd[:, :]))
            for i in range(node_tiles):
                rows = last_rows if i == node_tiles - 1 else P
                y = y_all[0:rows, i, :]
                nc.vector.tensor_scalar(y, y, moments[0:rows, 2 * i:2 * i + 1], rstd[0:rows, i:i + 1],
                                        ALU.subtract, ALU.mult).then_inc(s_norm, 1)

        @block.tensor
        def _(pe):
            pe.sem_inc(s_agg, NG)
            pe.sem_inc(s_hid_mm, 2)
            pe.wait_ge(s_lin1, 1)
            for i in range(node_tiles):
                n0 = i * P
                if n0 in X_SPLIT:
                    pe.wait_ge(s_x[X_SPLIT.index(n0)], 32)
                if i >= 4:
                    pe.wait_ge(s_h_sb, i - 3)
                o = w_ps[i % 4]
                nc.tensor.matmul(o[:, 0:3 * V_CH], xs[:, n0:n0 + P], w_of((0, S_CH), C_L1S, 3 * V_CH),
                                 start=True, stop=False, skip_group_check=True)
                nc.tensor.matmul(o[:, S_CH:FEAT], xv[:, n0:n0 + P], w_of((0, 3 * V_CH), C_L1V, 3 * V_CH),
                                 start=False, stop=True, skip_group_check=True).then_inc(s_h_mm, 1)
            pe.wait_ge(s_diag, 1)
            nc.tensor.matmul(hidden_ps[:, 0:2 * n_units], ones[0:n_units, :], diag[:, :], start=True, stop=True)\
              .then_inc(s_rows, 1)

            def hidden_half(k, half, first=False):
                a, b = ((0, HALF_COLS), (HALF_COLS, UNIT))[half]
                if half == 0:
                    pe.wait_ge(s_edges, k * 16 + 16)
                if half or not first:
                    pe.wait_ge(s_hid, k * 2 + half)
                nc.tensor.matmul(hidden_ps[:, 0:b - a], w_of((0, P), C_W1, P), edges[:, a:b], start=True, stop=True)\
                  .then_inc(s_hid_mm, 1)

            def mlp(it, g):
                ab, ts = GROUPS[g]
                pe.wait_ge(s_split, it * 2 + (1 + g // 4))
                pe.wait_ge(s_prod, it * NG + (g + 5))
                for k, t in enumerate(ts):
                    for part in (w2_high, w2_low):
                        last = nc.tensor.matmul(w_ps[g % 4][:, k * W_COLS:(k + 1) * W_COLS],
                                                hidden_parts[:, ab * UNIT + t * P:ab * UNIT + (t + 1) * P],
                                                part[:, :], start=part is w2_high, stop=part is w2_low)
                last.then_inc(s_w, 1)

            def sum_group(it, g):
                ab, ts = GROUPS[g]
                if g % 4 == 0:
                    pe.wait_ge(s_sel, it * 2 + (1 + g // 4))
                if g < 2:
                    pe.wait_ge(s_copied[ab], it + 1)
                pe.wait_ge(s_prod, it * NG + (NG + g + 1))
                for k, t in enumerate(ts):
                    j = FIRST[g] + k
                    last = nc.tensor.matmul(sums_ps[ab][:, 0:PROD], selector[:, j * P:(j + 1) * P],
                                            products[:, g, k, :], start=(t == 0), stop=(t == TILES - 1))
                last.then_inc(s_agg, 1)

            def turn(it, u):
                pe.wait_ge(s_copied[u], it + 1)
                pe.wait_ge(s_added, it * 2 + (u + 2))
                nc.tensor.transpose(turned[:, 0:P], sums_sb[:, u, 0:2 * S_CH], ident[:, :])
                for i in range(3):
                    c0 = 2 * S_CH + i * 3 * V_CH
                    last = nc.tensor.transpose(turned[0:3 * V_CH, (i + 1) * P:(i + 2) * P],
                                               sums_sb[:, u, c0:c0 + 3 * V_CH], ident[:, :])
                last.then_inc(s_turned, 1)

            pe.wait_ge(s_ctl, 1)
            hidden_half(0, 0, True)
            hidden_half(0, 1, True)
            pe.wait_ge(s_w2, 1)
            for g in range(3):
                mlp(0, g)
            n_it = pe.value_load(passes_i[0:1, pairs:pairs + 1], min_val=pairs, max_val=pairs * max_passes)
            with pe.Fori(0, n_it) as it:
                mlp(it, 3)
                hidden_half(it + 1, 0)
                sum_group(it, 0)
                turn(it, 0)
                mlp(it, 4)
                sum_group(it, 1)
                mlp(it, 5)
                sum_group(it, 2)
                mlp(it, 6)
                turn(it, 1)
                mlp(it, 7)
                sum_group(it, 3)
                sum_group(it, 4)
                mlp(it + 1, 0)
                hidden_half(it + 1, 1)
                sum_group(it, 5)
                sum_group(it, 6)
                mlp(it + 1, 1)
                sum_group(it, 7)
                mlp(it + 1, 2)
            turn(n_it, 0)
            turn(n_it, 1)

            pe.wait_ge(s_added, n_it * 2 + 4)
            pe.wait_ge(s_out_w, 1)
            pe.wait_ge(s_xsum, 4 * 16)
            for i in range(node_tiles):
                if i >= 4:
                    pe.wait_ge(s_yv, i - 3)
                o = w_ps[i % 4]
                n0 = i * P
                terms = [(sums_1[:, n0:n0 + P], w_of((0, P), C_A, O_S), 0)]
                for c in range(3):
                    m0 = 2 * c * NN + n0
                    terms.append((sums_v[:, m0:m0 + P], w_of((0, P), C_V + c * O_ALL, O_ALL), 0))
                for k in range(3):
                    m0 = (5 - 2 * k) * NN + n0
                    terms.append((sums_v[0:3 * V_CH, m0:m0 + P],
                                  w_of((0, 3 * V_CH), C_C + k * 3 * V_CH, 3 * V_CH), O_S))
                for n, (lhs, rhs, col) in enumerate(terms):
                    last = nc.tensor.matmul(o[:, col:col + rhs.shape[1]], lhs, rhs, start=(n == 0),
                                            stop=(n == len(terms) - 1), skip_group_check=True)
                last.then_inc(s_fin, 1)


def kernel(x, src, dst, edge_attr_4, edge_attr_64, node_vec1, L0_gnn_lin1_ws, L0_gnn_lin1_wv, L0_gnn_fc_w1,
           L0_gnn_fc_w2, L0_gnn_sc_ws, L0_gnn_sc_wv, L0_gnn_lin2_ws, L0_gnn_lin2_wv):
    import concourse.bacc as bacc
    from concourse.bass_utils import run_bass_kernel_spmd

    arr = lambda a: np.ascontiguousarray(a)
    x, src, dst, e4, e64, a = map(arr, (x, src, dst, edge_attr_4, edge_attr_64, node_vec1))
    w1, w2 = arr(L0_gnn_fc_w1), arr(L0_gnn_fc_w2)
    l1s, l1v, scs, scv = map(arr, (L0_gnn_lin1_ws, L0_gnn_lin1_wv, L0_gnn_sc_ws, L0_gnn_sc_wv))
    l2s, l2v = map(arr, (L0_gnn_lin2_ws, L0_gnn_lin2_wv))
    n, e = x.shape[0], src.shape[0]
    tiles = math.ceil((n + 1) / P)
    NN = tiles * P
    pairs = math.ceil(e / (2 * UNIT))
    e_pad = pairs * 2 * UNIT

    def padded(v, fill=0):
        out = np.full((e_pad,) + v.shape[1:], fill, v.dtype)
        out[:e] = v
        return out

    def by_tile(v):
        v = v.reshape((pairs, 2, TILES, P) + v.shape[1:])
        v = np.stack([v[:, ab, t] for ab, t in ORDER], axis=1)
        return np.ascontiguousarray(np.swapaxes(v, 1, 2))

    src_t = by_tile(padded(src))
    dst_p = padded(dst, n)
    dst_t = np.ascontiguousarray(by_tile(dst_p).transpose(1, 0, 2)).reshape(P, pairs * SLOTS)
    attr_t = np.ascontiguousarray(by_tile(padded(e4)).transpose(1, 0, 2, 3)).reshape(P, pairs * SLOTS * COMP)
    edges = np.ascontiguousarray(padded(e64).reshape(pairs, 2, UNIT, HID).transpose(0, 1, 3, 2))\
        .reshape(pairs, 2 * HID, UNIT)

    xs = np.zeros((S_CH, NN), x.dtype)
    xs[:, :n] = x[:, :S_CH].T
    xv = np.zeros((3 * V_CH, NN), x.dtype)
    xv[:, :n] = x[:, S_CH:].reshape(n, V_CH, 3).transpose(2, 1, 0).reshape(3 * V_CH, n)
    node = np.zeros((NN,), a.dtype)
    node[:n] = a[:, 0]
    node = np.ascontiguousarray(node.reshape(tiles, P).T)

    w = np.zeros((P, W_PACK), w1.dtype)
    for u in (0, 1):
        w[u * HID:(u + 1) * HID, C_W1 + u * HID:C_W1 + (u + 1) * HID] = w1
        w[u * HID:(u + 1) * HID, C_W2:C_W2 + W_COLS] = w2
    w[:S_CH, C_L1S:C_L1S + S_CH] = l1s
    w[:S_CH, C_A:C_V] = l2s[:S_CH]
    w[S_CH:, C_A:C_V] = scs
    for i in range(3):
        own = slice(i * V_CH, (i + 1) * V_CH)
        w[own, C_L1V + i * V_CH:C_L1V + (i + 1) * V_CH] = l1v
        c, own_c = C_V + i * O_ALL, C_V + i * O_ALL + O_S + i * V_CH
        k = CROSS[2 * i][3]
        w[0:V_CH, own_c:own_c + V_CH] = l2v[S_CH:S_CH + V_CH]
        w[V_CH:2 * V_CH, c:c + O_S] = l2s[S_CH:]
        w[2 * V_CH:3 * V_CH, c + O_S + k * V_CH:c + O_S + (k + 1) * V_CH] = l2v[S_CH + V_CH:]
        w[3 * V_CH:, own_c:own_c + V_CH] = scv
        c = C_C + i * 4 * V_CH
        w[:S_CH, c:c + V_CH] = l2v[:S_CH]
        w[2 * V_CH:3 * V_CH, c:c + V_CH] = l2v[S_CH + V_CH:]

    arrays = {"xs": xs, "xv": xv, "x": x, "src": src_t, "dst_tiles": dst_t,
              "dst_units": dst_p.reshape(pairs * 2, UNIT), "attr": attr_t, "edges": edges, "node": node, "weights": w}
    nc = bacc.Bacc("TRN2", target_bir_lowering=False, num_devices=1)
    args = [nc.dram_tensor(f"{k}_dram", v.shape, mybir.dt.from_np(v.dtype), kind="ExternalInput").ap()
            for k, v in arrays.items()]
    out = nc.dram_tensor("out_dram", x.shape, F32, kind="ExternalOutput").ap()
    build(nc, *args, out, n)
    r = run_bass_kernel_spmd(nc, [{f"{k}_dram": v for k, v in arrays.items()}], core_ids=[0])
    return r.results[0]["out_dram"]
```

```python
import math

import numpy as np

import concourse.bass as bass
from concourse import mybir
from concourse.alu_op_type import AluOpType as ALU

F32 = mybir.dt.float32
F32R = mybir.dt.float32r
I32 = mybir.dt.int32
ACT = mybir.ActivationFunctionType
AX = mybir.AxisListType

P = 128
S_CH, V_CH = 64, 32
FEAT = S_CH + 3 * V_CH
HID = 64
W_COLS = 2 * S_CH + 3 * V_CH
O_S = 96
O_ALL = O_S + 3 * V_CH
COMP = 4
WINDOW = 32
PROD = 2 * S_CH + 9 * V_CH

TILES = 7
UNIT = TILES * P
STEPS = [(0, 1), (2, 3), (4, 5), (6,)]
GROUPS = [(ab, ts) for ts in STEPS for ab in (0, 1)]
NG = len(GROUPS)
ORDER = [(ab, t) for ab, ts in GROUPS for t in ts]
SLOTS = len(ORDER)
FIRST = [sum(len(ts) for _, ts in GROUPS[:g]) for g in range(NG)]
PAIR_ATTR = SLOTS * COMP
INDEX_COLS = [(FIRST[2 * q], FIRST[2 * q + 1] + len(STEPS[q])) for q in range(len(STEPS))]
HALF = FIRST[4]
HALVES = [(0, 4 * P), (4 * P, UNIT)]

C_PA = 0
C_PB = C_PA + P
C_W1 = C_PB + P
C_W2 = C_W1 + P
C_OUT = C_W2 + W_COLS
OUT_S = V_CH
OUT_V = (P, P + V_CH, 0)
TERMS = [(0, P), (OUT_S, P + V_CH), (OUT_S, P + V_CH), (0, P), (2 * V_CH, P), (2 * V_CH, P), (0, P)]
TERM_AT = [C_OUT + sum(n for _, n in TERMS[:t]) for t in range(len(TERMS))]
W_PACK = C_OUT + sum(n for _, n in TERMS)

CROSS = [(0, 2, -1, 1), (1, 0, -1, 2), (1, 2, 1, 0), (2, 0, 1, 1), (0, 1, 1, 2), (2, 1, -1, 0)]


def build(nc, xa_d, xb_d, x_d, src_d, dst_tiles_d, dst_units_d, attr_d, edges_d, node_d, weights_d, out_d, n_nodes):
    node_tiles = math.ceil((n_nodes + 1) / P)
    NN = node_tiles * P
    n_units = dst_units_d.shape[0]
    pairs = n_units // 2
    last_base = NN - WINDOW
    last_rows = n_nodes - (node_tiles - 1) * P
    max_passes = math.ceil((n_nodes + 1) / WINDOW)
    assert n_nodes <= last_base and 0 < last_rows <= P

    sb = lambda name, shape, dt=F32: nc.alloc_sbuf_tensor(name, shape, dt)
    sem = nc.alloc_semaphore

    weights = sb("weights", [P, W_PACK])
    node_attr = sb("node_attr", [P, node_tiles])
    attr = sb("attr", [P, (pairs + 1) * PAIR_ATTR])
    rel = sb("rel", [P, pairs * SLOTS])
    dst_tiles = sb("dst_tiles", [P, pairs * SLOTS], I32)
    dst_units = sb("dst_units", [n_units, UNIT], I32)
    edges = sb("edges", [P, UNIT])
    index = [sb(f"index{q}", [P, b - a], I32) for q, (a, b) in enumerate(INDEX_COLS)]
    ident = sb("ident", [P, P])
    ones = sb("ones", [P, P])
    iota = sb("iota", [P, WINDOW])
    sums_1 = sb("sums_1", [P, NN])
    sums_v = sb("sums_v", [P, 6 * NN])
    lo = sb("lo", [n_units, 1])
    hi = sb("hi", [n_units, 1])
    span = sb("span", [n_units, 1], I32)
    span_windows = sb("span_windows", [n_units, 1], I32)
    passes = sb("passes", [n_units, 1])
    diag = sb("diag", [n_units, 2 * n_units])
    unit_rows = sb("unit_rows", [P, 2 * n_units])
    pair_passes = sb("pair_passes", [P, pairs])
    total = sb("total", [P, 1])
    base_i = sb("base_i", [P, n_units], I32)
    passes_i = sb("passes_i", [P, pairs + 1], I32)

    ARENA = 2 * NN + node_tiles * FEAT
    arena = sb("arena", [P, ARENA])
    xa = arena[:, 0:NN]
    xb = arena[:, NN:2 * NN]
    h_all = arena[:, 2 * NN:].rearrange("p (i c) -> p i c", c=FEAT)
    at = [0]

    def cut(n):
        at[0] += n
        assert at[0] <= ARENA
        return arena[:, at[0] - n:at[0]]

    sums_sb = cut(2 * PROD).rearrange("p (u c) -> p u c", u=2)
    onehot = cut(SLOTS * WINDOW)
    y_at = at[0]
    gathered = cut(SLOTS * FEAT).rearrange("p (j c) -> p j c", c=FEAT)
    products = cut(NG * 2 * PROD).rearrange("p (g t c) -> p g t c", g=NG, t=2)
    y_all = arena[:, y_at:y_at + node_tiles * FEAT].rearrange("p (i c) -> p i c", c=FEAT)
    Y_FIRST = SLOTS
    selector = sb("selector", [P, SLOTS * P])
    hidden = sb("hidden", [P, UNIT])
    hidden_parts = sb("hidden_parts", [P, 2 * UNIT], F32R)
    w2_high = sb("w2_high", [P, W_COLS], F32R)
    w2_low = sb("w2_low", [P, W_COLS], F32R)
    small = sb("small", [P, 2 * O_S + 2 * FEAT + 2 * 6])
    eps = sb("eps", [P, 1])
    gate_sb = small[:, 0:2 * O_S].rearrange("p (s c) -> p s c", s=2)
    stage_y = small[:, 2 * O_S:2 * O_S + 2 * FEAT].rearrange("p (s c) -> p s c", s=2)
    bn = small[:, 2 * O_S + 2 * FEAT:].rearrange("p (s c) -> p s c", s=2)
    moments = sb("moments", [P, node_tiles * 2])
    std = sb("std", [P, node_tiles])

    banks = [nc.alloc_psum_tensor(f"bank{i}", [P, 512], F32) for i in range(8)]
    w_ps = banks[0:4]
    sums_ps = banks[4:6]
    turned_ps = banks[6]
    hidden_ps = banks[7]
    turned = turned_ps[:, :]
    last_turned_ps = hidden_ps
    out_ps = banks[0:6]

    table = nc.dram_tensor("h_table", [NN, FEAT], F32, kind="Internal").ap()

    X_SPLIT = (0, 4, 10, 17, node_tiles)
    TABLE_SPLIT = (0, 11, 21, node_tiles)
    WEIGHT_SPLIT = (0, C_W1, C_OUT, W_PACK)
    NORM_SPLIT = (0, 9, node_tiles - 8, node_tiles)

    s_weights = [sem(f"{what}_weights_loaded") for what in ("projection", "mlp", "output")]
    s_nodes = sem("node_attr_loaded")
    s_x = [sem(f"x_loaded{i}") for i in range(len(X_SPLIT) - 1)]
    s_dstu = sem("dst_units_loaded")
    s_dstt = sem("dst_tiles_loaded")
    s_attr = sem("attr_loaded")
    s_ones = sem("ones_made")
    s_const = sem("constants_made")
    s_const_step = sem("constant_steps")
    s_lin1 = sem("lin1_scaled")
    s_out_w = sem("output_weights_scaled")
    s_xb_zero = sem("x_b_rows_zeroed")
    s_h_mm = sem("h_multiplied")
    s_h_sb = sem("h_scaled")
    s_table = sem("table_stored")
    s_diag = sem("unit_diagonals_made")
    s_rows = sem("unit_rows_multiplied")
    s_ctl = sem("loop_counts_ready")
    s_chain = sem("vector_step_done")
    s_rel = sem("window_moved")
    s_edges = [sem(f"edges_half{i}_loaded") for i in range(2)]
    s_index = [sem(f"index{q}_loaded") for q in range(len(INDEX_COLS))]
    s_gather = [sem(f"tile{j}_gathered") for j in range(SLOTS)]
    s_slot = sem("gather_slots_free")
    s_hid_mm = sem("hidden_multiplied")
    s_hid = sem("hidden_high_part_ready")
    s_split = sem("hidden_low_part_ready")
    s_w2 = sem("w2_split")
    s_w = sem("mlp_weights_ready")
    s_prod = sem("products_ready")
    s_onehot = sem("onehot_ready")
    s_sel = sem("selector_ready")
    s_agg = sem("group_summed")
    s_copied = [sem("sums_a_copied"), sem("sums_b_copied")]
    s_turned = sem("sums_transposed")
    s_added = sem("sums_added")
    s_zeroed = sem("accumulators_zeroed")
    s_xsum = sem("x_placed_in_accumulators")
    s_xr = [sem("first_x_rows_loaded"), sem("last_x_rows_loaded")]
    s_fin = sem("output_multiplied")
    s_gate = sem("gate_ready")
    s_yv = sem("residual_ready")
    s_mom = sem("moments_ready")
    s_std = sem("std_ready")
    s_rstd = sem("reciprocal_of_std_ready")
    s_norm = sem("rows_normalised_by_gpsimd")
    s_norm_v = sem("rows_normalised_by_vector")
    s_out = sem("output_stored")

    def w_of(rows, col, n):
        return weights[rows[0]:rows[1], col:col + n]

    def passes_of(eng, v):
        return eng.value_load(passes_i[0:1, bass.ds(v, 1)], min_val=1, max_val=max_passes)

    def counted(eng, reg):
        return eng.snap(reg, min_val=0, max_val=pairs * max_passes)

    WARM_UP = 8
    STORE_SPLIT = (0, 9, node_tiles - 8, node_tiles - 4, node_tiles - 1)
    NORM_DVE = node_tiles - 6

    def batch_parts(a, b):
        if b < node_tiles:
            return [(P, a, b)]
        return [(P, a, b - 1), (last_rows, b - 1, b)]

    def normalise(eng, i):
        rows = last_rows if i == node_tiles - 1 else P
        y = y_all[0:rows, i, :]
        return eng.tensor_scalar(y, y, moments[0:rows, 2 * i:2 * i + 1], std[0:rows, i:i + 1],
                                 ALU.subtract, ALU.mult)

    with nc.Block() as block:

        @block.sync
        def _(sp):
            def load_weights(k):
                a, b = WEIGHT_SPLIT[k:k + 2]
                sp.dma_start(weights[:, a:b], weights_d[:, a:b]).then_inc(s_weights[k], 16)

            def load_x(k):
                a, b = (t * P for t in X_SPLIT[k:k + 2])
                sp.dma_start(xa[:, a:b], xa_d[:, a:b]).then_inc(s_x[k], 16)
                sp.dma_start(xb[3 * V_CH:P, a:b], xb_d[:, a:b]).then_inc(s_x[k], 16)

            load_weights(0)
            load_x(0)
            load_x(1)
            sp.dma_start(dst_units[:, :], dst_units_d).then_inc(s_dstu, 16)
            load_x(2)
            load_x(3)
            load_weights(1)
            sp.dma_start(dst_tiles[:, :], dst_tiles_d).then_inc(s_dstt, 16)
            load_weights(2)
            sp.dma_start(attr[:, 0:PAIR_ATTR], attr_d[:, 0:PAIR_ATTR]).then_inc(s_attr, 16)
            sp.wait_ge(s_ctl, 1)
            with sp.register("sync_iteration") as reg:
                sp.reg_mov(reg, 0)
                with sp.Fori(0, pairs) as v:
                    n = passes_of(sp, v)
                    with sp.Fori(0, n):
                        it = counted(sp, reg)
                        for half, (a, b) in enumerate(HALVES):
                            sp.wait_ge(s_hid_mm, it * 2 + (half + 1))
                            sp.dma_start(edges[:, a:b],
                                         edges_d[bass.ds(v, 1), :, a:b].rearrange("a p n -> (a p) n"))\
                              .then_inc(s_edges[half], 16)
                        for q, (a, b) in enumerate(INDEX_COLS):
                            sp.wait_ge(s_prod, it * NG + 2 * (q + 1))
                            sp.dma_start(index[q][:, :],
                                         src_d[bass.ds(v, 1), :, a:b].rearrange("a p n -> (a p) n"))\
                              .then_inc(s_index[q], 16)
                        sp.reg_add(reg, reg, 1)
                    c = bass.ds((v + 1) * PAIR_ATTR, PAIR_ATTR)
                    sp.dma_start(attr[:, c], attr_d[:, c]).then_inc(s_attr, 16)
                it = counted(sp, reg)
                for half, (a, b) in enumerate(HALVES):
                    sp.wait_ge(s_hid_mm, it * 2 + (half + 1))
                    sp.dma_start(edges[:, a:b], edges_d[pairs - 1, :, a:b]).then_inc(s_edges[half], 16)
                sp.dma_start(sums_1[S_CH:P, :], xa_d[0:S_CH, :]).then_inc(s_xsum, 16)
                for i, v_i in enumerate((xa_d[S_CH:S_CH + V_CH, :], xa_d[S_CH + V_CH:P, :], xb_d)):
                    sp.dma_start(sums_v[3 * V_CH:P, 2 * i * NN:(2 * i + 1) * NN], v_i).then_inc(s_xsum, 16)
                sp.wait_ge(s_prod, it * NG + NG)
                sp.dma_start(y_all[:, 0:Y_FIRST, :], x_d[0:Y_FIRST * P, :].rearrange("(i p) c -> p i c", p=P))\
                  .then_inc(s_xr[0], 16)
                sp.wait_ge(s_agg, it * NG + NG)
            full = node_tiles - 1
            sp.dma_start(y_all[:, Y_FIRST:full, :],
                         x_d[Y_FIRST * P:full * P, :].rearrange("(i p) c -> p i c", p=P)).then_inc(s_xr[1], 16)
            sp.dma_start(y_all[0:last_rows, full, :], x_d[full * P:n_nodes, :]).then_inc(s_xr[1], 16)
            for a, b in zip(STORE_SPLIT, STORE_SPLIT[1:]):
                sp.wait_ge(s_norm, min(b, NORM_DVE))
                if b > NORM_DVE:
                    sp.wait_ge(s_norm_v, b - NORM_DVE)
                sp.dma_start(out_d[a * P:b * P, :].rearrange("(i p) c -> p i c", p=P), y_all[:, a:b, :])\
                  .then_inc(s_out, 16)
            sp.wait_ge(s_norm_v, node_tiles - NORM_DVE)
            sp.dma_start(out_d[full * P:n_nodes, :], y_all[0:last_rows, full, :]).then_inc(s_out, 16)
            sp.wait_ge(s_out, len(STORE_SPLIT) * 16)

        @block.gpsimd
        def _(pool):
            pool.memset(ones[:, :], 1.0).then_inc(s_ones, 1)
            pool.memset(xb[0:3 * V_CH, :], 0.0).then_inc(s_xb_zero, 1)
            pool.memset(eps[:, :], 1e-5).then_inc(s_const, 1)
            pool.memset(ident[:, :], 0.0).then_inc(s_const_step, 1)
            pool.wait_ge(s_const_step, 1)
            pool.affine_select(out=ident[:, :], in_=ident[:, :], compare_op=ALU.not_equal, fill=1.0, base=0,
                               pattern=[[-1, P]], channel_multiplier=1).then_inc(s_const, 1)
            pool.iota(iota[:, :], pattern=[[1, WINDOW]], base=0, channel_multiplier=0,
                      allow_small_or_imprecise_dtypes=True).then_inc(s_const, 1)
            pool.memset(sums_v[0:3 * V_CH, :], 0.0).then_inc(s_zeroed, 1)
            pool.wait_ge(s_ctl, 1)
            with pool.register("pool_iteration") as reg:
                pool.reg_mov(reg, 0)
                with pool.Fori(0, pairs) as v:
                    n = passes_of(pool, v)
                    with pool.Fori(0, n):
                        it = counted(pool, reg)
                        for g, (ab, ts) in enumerate(GROUPS):
                            if g % 2 == 0:
                                pool.wait_ge(s_index[g // 2], it * 16 + 16)
                            pool.wait_ge(s_prod, it * NG + (g + 1))
                            pool.sem_inc(s_slot, 1)
                            for j in range(FIRST[g], FIRST[g] + len(ts)):
                                col = j - INDEX_COLS[g // 2][0]
                                pool.wait_ge(s_table, 3 * 16)
                                pool.indirect_dma_start(
                                    out=gathered[:, j, :], out_offset=None, in_=table,
                                    in_offset=bass.IndirectOffsetOnAxis(ap=index[g // 2][:, col:col + 1], axis=0))\
                                    .then_inc(s_gather[j], 16)
                        pool.reg_add(reg, reg, 1)
            for b in range(len(NORM_SPLIT) - 1):
                pool.wait_ge(s_rstd, b + 1)
                for i in range(NORM_SPLIT[b], min(NORM_SPLIT[b + 1], NORM_DVE)):
                    normalise(nc.gpsimd, i).then_inc(s_norm, 1)

        @block.scalar
        def _(act):
            act.dma_start(node_attr[:, :], node_d).then_inc(s_nodes, 16)
            act.wait_ge(s_nodes, 16)
            for i in range(node_tiles):
                act.wait_ge(s_h_mm, i + 1)
                nc.scalar.activation(h_all[:, i, :], w_ps[i % 4][:, 0:FEAT], ACT.Copy, scale=node_attr[:, i:i + 1])\
                  .then_inc(s_h_sb, 1)
                if i + 1 in TABLE_SPLIT:
                    a = TABLE_SPLIT[TABLE_SPLIT.index(i + 1) - 1]
                    act.wait_ge(s_h_sb, i + 1)
                    act.dma_start(table[a * P:(i + 1) * P, :].rearrange("(i p) c -> p i c", p=P),
                                  h_all[:, a:i + 1, :]).then_inc(s_table, 16)

            def silu(k, half, first):
                a, b = HALVES[half]
                act.wait_ge(s_hid_mm, k * 2 + (half + 3))
                if not first:
                    act.wait_ge(s_w, (k - 1) * NG + 4 * (half + 1))
                    act.wait_ge(s_split, (k - 1) * 2 + (half + 1))
                nc.scalar.activation(hidden[:, a:b], hidden_ps[:, 0:b - a], ACT.Silu, scale=1 / math.sqrt(HID))
                for u in (0, 1):
                    r = slice(u * HID, (u + 1) * HID)
                    last = nc.scalar.activation(hidden_parts[r, u * UNIT + a:u * UNIT + b], hidden_ps[r, 0:b - a],
                                                ACT.Silu, scale=1 / math.sqrt(HID))
                last.then_inc(s_hid, 1)

            silu(0, 0, True)
            silu(0, 1, True)
            act.wait_ge(s_ctl, 1)
            n_it = act.value_load(passes_i[0:1, pairs:pairs + 1], min_val=pairs, max_val=pairs * max_passes)
            with act.Fori(0, n_it) as it:
                silu(it + 1, 0, False)
                silu(it + 1, 1, False)
                for u in (0, 1):
                    act.wait_ge(s_agg, it * NG + (2 * NG - 1 + u))
                    act.wait_ge(s_turned, it * 2 + (u + 1))
                    nc.scalar.activation(sums_sb[:, u, :], sums_ps[u][:, 0:PROD], ACT.Copy)\
                      .then_inc(s_copied[u], 1)
            for i in range(node_tiles):
                rows = last_rows if i == node_tiles - 1 else P
                act.wait_ge(s_fin, i + 1)
                if i >= 2:
                    act.wait_ge(s_yv, i - 1)
                nc.scalar.activation(gate_sb[0:rows, i % 2, :], out_ps[i % len(out_ps)][0:rows, OUT_S:OUT_S + O_S],
                                     ACT.Sigmoid, scale=node_attr[0:rows, i:i + 1]).then_inc(s_gate, 1)
                if i + 1 == node_tiles or i in NORM_SPLIT[1:]:
                    b = node_tiles if i + 1 == node_tiles else i
                    a = NORM_SPLIT[NORM_SPLIT.index(b) - 1]
                    act.wait_ge(s_mom, b)
                    variance = moments[:, :].rearrange("p (i m) -> p i m", m=2)[:, :, 1]
                    for r, lo_tile, hi_tile in batch_parts(a, b):
                        last = nc.scalar.activation(std[0:r, lo_tile:hi_tile], variance[0:r, lo_tile:hi_tile],
                                                    ACT.Sqrt, bias=eps[0:r, :])
                    last.then_inc(s_std, 1)

        @block.vector
        def _(dve):
            chain = [0]

            def link(ins):
                chain[0] += 1
                ins.then_inc(s_chain, 1)
                dve.wait_ge(s_chain, chain[0])

            def scale(rows, col, n, by):
                w = w_of(rows, col, n)
                return nc.vector.tensor_scalar(w, w, by, None, ALU.mult)

            dve.sem_inc(s_prod, NG)
            dve.sem_inc(s_added, 2)
            dve.wait_ge(s_weights[0], 16)
            scale((0, S_CH), C_PA, P, 1 / math.sqrt(S_CH))
            scale((S_CH, P), C_PA, P, 1 / math.sqrt(V_CH))
            scale((3 * V_CH, P), C_PB, P, 1 / math.sqrt(V_CH)).then_inc(s_lin1, 1)

            dve.wait_ge(s_dstu, 16)
            nc.vector.tensor_reduce(lo[:, :], dst_units[:, :], AX.X, ALU.min)
            link(nc.vector.tensor_reduce(hi[:, :], dst_units[:, :], AX.X, ALU.max))
            link(nc.vector.tensor_tensor(span[:, :], hi[:, :], lo[:, :], ALU.subtract))
            link(nc.vector.tensor_scalar(span_windows[:, :], span[:, :], int(math.log2(WINDOW)), None,
                                         ALU.logical_shift_right))
            link(nc.vector.tensor_scalar(passes[:, :], span_windows[:, :], 1.0, None, ALU.add))
            dve.wait_ge(s_const, 3)
            eye = ident[0:n_units, 0:n_units]
            nc.vector.tensor_scalar(diag[:, 0:n_units], eye, lo[:, 0:1], None, ALU.mult)
            nc.vector.tensor_scalar(diag[:, n_units:], eye, passes[:, 0:1], None, ALU.mult).then_inc(s_diag, 1)
            dve.wait_ge(s_weights[1], 16)
            w2 = w_of((0, P), C_W2, W_COLS)
            link(nc.vector.tensor_copy(w2_high[:, :], w2))
            nc.vector.tensor_tensor(w2_low[:, :], w2, w2_high[:, :].bitcast(F32), ALU.subtract).then_inc(s_w2, 1)
            dve.wait_ge(s_rows, 1)
            link(nc.vector.tensor_copy(unit_rows[:, :], turned[:, 0:2 * n_units]))
            by_pair = unit_rows[:, n_units:].rearrange("p (v u) -> p v u", u=2)
            link(nc.vector.tensor_tensor(pair_passes[:, :], by_pair[:, :, 0], by_pair[:, :, 1], ALU.max))
            link(nc.vector.tensor_reduce(total[:, :], pair_passes[:, :], AX.X, ALU.add))
            nc.vector.tensor_copy(base_i[:, :], unit_rows[:, 0:n_units])
            nc.vector.tensor_copy(passes_i[:, 0:pairs], pair_passes[:, :])
            link(nc.vector.tensor_copy(passes_i[:, pairs:], total[:, :]))
            dve.sem_inc(s_ctl, 1)

            dve.wait_ge(s_dstt, 16)
            rel_v = rel[:, :].rearrange("p (v j) -> p v j", j=SLOTS)
            dst_v = dst_tiles[:, :].rearrange("p (v j) -> p v j", j=SLOTS)
            starts = unit_rows[:, 0:n_units].rearrange("p (v u) -> p v u", u=2)
            for u in (0, 1):
                quads = slice(0, 12)
                r = rel_v[:, :, quads].rearrange("p v (q u t) -> p v q u t", u=2, t=2)[:, :, :, u, :]
                d = dst_v[:, :, quads].rearrange("p v (q u t) -> p v q u t", u=2, t=2)[:, :, :, u, :]
                m = starts[:, :, u:u + 1].rearrange("p v (a b) -> p v a b", b=1).to_broadcast([P, pairs, 3, 2])
                nc.vector.tensor_tensor(r, d, m, ALU.subtract)
            link(nc.vector.tensor_tensor(rel_v[:, :, 12:14], dst_v[:, :, 12:14], starts, ALU.subtract))
            dve.sem_inc(s_rel, 1)

            dve.wait_ge(s_weights[2], 16)
            c = 1 / math.sqrt(HID) / math.sqrt(16.0)
            width = lambda a, b: sum(n for _, n in TERMS[a:b])
            scale((0, S_CH), TERM_AT[0], width(0, 1), c / math.sqrt(96.0))
            scale((S_CH, P), TERM_AT[0], width(0, 1), 1 / math.sqrt(S_CH))
            scale((0, V_CH), TERM_AT[1], width(1, 4), c / math.sqrt(128.0))
            scale((V_CH, 2 * V_CH), TERM_AT[1], width(1, 4), c / math.sqrt(96.0) / math.sqrt(3.0))
            scale((3 * V_CH, P), TERM_AT[1], width(1, 4), 1 / math.sqrt(V_CH))
            scale((0, 2 * V_CH), TERM_AT[4], width(4, 7), c / math.sqrt(128.0))
            rows = (2 * V_CH, 3 * V_CH)
            c3 = c / math.sqrt(128.0) / math.sqrt(2.0)
            for i in range(3):
                scale(rows, TERM_AT[1 + i], width(1 + i, 2 + i), CROSS[2 * i][2] * c3)
            for k in range(3):
                last = scale(rows, TERM_AT[4 + k], width(4 + k, 5 + k), CROSS[5 - 2 * k][2] * c3)
            last.then_inc(s_out_w, 1)
            nc.vector.memset(sums_1[0:S_CH, :], 0.0).then_inc(s_zeroed, 1)
            dve.wait_ge(s_h_mm, node_tiles)
            nc.vector.memset(sums_sb[:, 0, :], 0.0).then_inc(s_copied[0], 1)
            nc.vector.memset(sums_sb[:, 1, :], 0.0).then_inc(s_copied[1], 1)

            def multiply(it, g):
                ab, ts = GROUPS[g]
                n, j0 = len(ts), FIRST[g]
                w = w_ps[g % 4]
                dve.wait_ge(s_w, it * NG + (g + 1))
                dve.wait_ge(s_agg, it * NG + (g + 1))
                for k in range(n):
                    dve.wait_ge(s_gather[j0 + k], it * 16 + 16)
                wv = w[:, 0:n * W_COLS].rearrange("p (t c) -> p t c", t=n)
                es = gathered[:, j0:j0 + n, 0:S_CH].rearrange("p t (a c) -> p t a c", a=1)\
                    .to_broadcast([P, n, 2, S_CH])
                nc.vector.tensor_tensor(
                    products[:, g, 0:n, 0:2 * S_CH].rearrange("p t (a c) -> p t a c", a=2),
                    wv[:, :, 0:2 * S_CH].rearrange("p t (a c) -> p t a c", a=2), es, ALU.mult)
                for k in range(n):
                    kinds = wv[:, k, 2 * S_CH:].rearrange("p (i a c) -> p i a c", i=1, a=3)\
                        .to_broadcast([P, 3, 3, V_CH])
                    ev = gathered[:, j0 + k, S_CH:].rearrange("p (i a c) -> p i a c", i=3, a=1)\
                        .to_broadcast([P, 3, 3, V_CH])
                    last = nc.vector.tensor_tensor(
                        products[:, g, k, 2 * S_CH:].rearrange("p (i a c) -> p i a c", i=3, a=3),
                        kinds, ev, ALU.mult)
                last.then_inc(s_prod, 1)

            def split(k, half):
                a, b = HALVES[half]
                dve.wait_ge(s_hid, k * 2 + (half + 1))
                for u in (0, 1):
                    own, other = (slice(x * HID, (x + 1) * HID) for x in (u, 1 - u))
                    last = nc.vector.tensor_tensor(
                        hidden_parts[other, u * UNIT + a:u * UNIT + b], hidden[own, a:b],
                        hidden_parts[own, u * UNIT + a:u * UNIT + b].bitcast(F32), ALU.subtract)
                last.then_inc(s_split, 1)

            def hot_of(half):
                n = (HALF, SLOTS - HALF)[half]
                hot = onehot[:, half * HALF * WINDOW:(half * HALF + n) * WINDOW]
                return n, hot.rearrange("p (j n) -> p j n", n=WINDOW)

            def point(it, v, half):
                n, hot = hot_of(half)
                r = rel[:, bass.ds(v * SLOTS + half * HALF, n)].rearrange("p (j n) -> p j n", n=1)\
                    .to_broadcast([P, n, WINDOW])
                io = iota[:, :].rearrange("p (j n) -> p j n", j=1).to_broadcast([P, n, WINDOW])
                dve.wait_ge(s_rel, it + 1)
                nc.vector.tensor_tensor(hot, io, r, ALU.is_equal).then_inc(s_onehot, 1)

            def select(it, v, half):
                n, hot = hot_of(half)
                a = half * HALF
                dve.wait_ge(s_onehot, it * 2 + (half + 1))
                dve.wait_ge(s_attr, v * 16 + 16)
                dve.wait_ge(s_agg, it * NG + 4 * (half + 1))
                e = attr[:, bass.ds((v * SLOTS + a) * COMP, n * COMP)].rearrange("p (j k n) -> p j k n", k=COMP, n=1)\
                    .to_broadcast([P, n, COMP, WINDOW])
                nc.vector.tensor_tensor(
                    selector[:, a * P:(a + n) * P].rearrange("p (j k n) -> p j k n", k=COMP, n=WINDOW),
                    hot.rearrange("p j (k n) -> p j k n", k=1).to_broadcast([P, n, COMP, WINDOW]), e, ALU.mult)\
                    .then_inc(s_sel, 1)

            def add_sums(it, u, base, bank=turned_ps):
                dve.wait_ge(s_turned, it * 2 + (u + 1))
                dve.wait_ge(s_added, it * 2 + (u + 2))

                def add(tensor, r0, src0, rows, set0, set_step, n_sets, off, stride):
                    ps = bass.AP(bank, src0 * 512 + off, [[512, rows], [stride, n_sets], [1, WINDOW]])
                    acc = tensor[r0:r0 + rows, :].rearrange("p (s n) -> p s n", n=NN)\
                        [:, set0:set0 + set_step * (n_sets - 1) + 1:set_step, bass.ds(base, WINDOW)]
                    return nc.vector.tensor_tensor(acc, ps, acc, ALU.add)

                k0 = WINDOW
                add(sums_1, 0, 0, S_CH, 0, 1, 1, 0, P)
                add(sums_v, 0, S_CH, S_CH, 1, 2, 3, k0 + 2 * WINDOW, -WINDOW)
                add(sums_v, 0, 0, V_CH, 0, 2, 3, P, P)
                add(sums_v, V_CH, V_CH, V_CH, 0, 2, 3, P + k0, P + WINDOW)
                add(sums_v, 2 * V_CH, 2 * V_CH, V_CH, 0, 1, 4, P + k0 + 2 * WINDOW, 2 * WINDOW)
                add(sums_v, 2 * V_CH, 2 * V_CH, V_CH, 4, 1, 2, P + k0 + WINDOW, 2 * P).then_inc(s_added, 1)

            split(0, 0)
            dve.wait_ge(s_zeroed, 2)
            with dve.register("vector_iteration") as reg, dve.register("window_a") as window_a, \
                    dve.register("window_b") as window_b:
                windows = (window_a, window_b)
                dve.reg_mov(reg, 0)
                for w in windows:
                    dve.reg_mov(w, 0)
                at_node = lambda u: dve.snap(windows[u], min_val=0, max_val=last_base)

                def move_window(v, u, j):
                    start = dve.value_load(base_i[0:1, bass.ds(v * 2 + u, 1)], min_val=0, max_val=n_nodes)
                    dve.reg_alu(windows[u], start + j * WINDOW, last_base, ALU.min)

                with dve.Fori(0, pairs) as v:
                    n = passes_of(dve, v)
                    with dve.Fori(0, n) as j:
                        it = counted(dve, reg)
                        point(it, v, 0)
                        split(it, 1)
                        select(it, v, 0)
                        multiply(it, 0)
                        point(it, v, 1)
                        multiply(it, 1)
                        add_sums(it, 0, at_node(0))
                        multiply(it, 2)
                        move_window(v, 0, j)
                        select(it, v, 1)
                        multiply(it, 3)
                        add_sums(it, 1, at_node(1))
                        split(it + 1, 0)
                        move_window(v, 1, j)
                        multiply(it, 4)
                        multiply(it, 5)
                        r = rel[:, bass.ds(v * SLOTS, SLOTS)]
                        nc.vector.tensor_scalar(r, r, -float(WINDOW), None, ALU.add).then_inc(s_rel, 1)
                        multiply(it, 6)
                        multiply(it, 7)
                        dve.reg_add(reg, reg, 1)
                it = counted(dve, reg)
                add_sums(it, 0, at_node(0))
                add_sums(it, 1, at_node(1), last_turned_ps)

            for i in range(node_tiles):
                if i == 0:
                    dve.wait_ge(s_xr[0], 16)
                if i == Y_FIRST:
                    dve.wait_ge(s_xr[1], 32)
                rows = last_rows if i == node_tiles - 1 else P
                a = node_attr[0:rows, i:i + 1]
                o = out_ps[i % len(out_ps)]
                gate = gate_sb[0:rows, i % 2, :]
                t = stage_y[0:rows, i % 2, :]
                dve.wait_ge(s_gate, i + 1)
                nc.vector.scalar_tensor_tensor(out=t[:, 0:S_CH], in0=o[0:rows, OUT_S:OUT_S + S_CH], scalar=a,
                                               in1=gate[:, 0:S_CH], op0=ALU.mult, op1=ALU.mult)
                vectors = t[:, S_CH:].rearrange("p (d k) -> p k d", k=3)
                for k, n in ((0, 2), (2, 1)):
                    last = nc.vector.scalar_tensor_tensor(
                        out=vectors[:, k:k + n, :],
                        in0=o[0:rows, OUT_V[k]:OUT_V[k] + n * V_CH].rearrange("p (k d) -> p k d", k=n), scalar=a,
                        in1=gate[:, S_CH:].rearrange("p (k d) -> p k d", k=1).to_broadcast([rows, n, V_CH]),
                        op0=ALU.mult, op1=ALU.mult)
                link(last)
                y = y_all[0:rows, i, :]
                nc.vector.tensor_tensor(y, y, t, ALU.add).then_inc(s_yv, 1)
                dve.wait_ge(s_yv, i + 1)
                link(nc.vector.bn_stats(bn[0:rows, i % 2, :], y))
                nc.vector.bn_aggr(moments[0:rows, 2 * i:2 * i + 2], bn[0:rows, i % 2, :]).then_inc(s_mom, 1)
                if i + 1 == node_tiles or i - 1 in NORM_SPLIT[1:]:
                    b = NORM_SPLIT.index(node_tiles if i + 1 == node_tiles else i - 1)
                    dve.wait_ge(s_std, b)
                    for r, a, z in batch_parts(NORM_SPLIT[b - 1], NORM_SPLIT[b]):
                        last = nc.vector.reciprocal(std[0:r, a:z], std[0:r, a:z])
                    last.then_inc(s_rstd, 1)
                    if NORM_SPLIT[b] > NORM_DVE:
                        dve.wait_ge(s_rstd, b)
                        for j in range(NORM_DVE, NORM_SPLIT[b]):
                            normalise(nc.vector, j).then_inc(s_norm_v, 1)

        @block.tensor
        def _(pe):
            pe.sem_inc(s_agg, NG)
            pe.sem_inc(s_hid_mm, 2)
            UNIT_ROWS_AFTER = node_tiles // 2
            pe.wait_ge(s_ones, 1)
            for _ in range(WARM_UP):
                nc.tensor.matmul(turned[:, 0:P], ones[:, :], ones[:, :], start=True, stop=True)
            pe.wait_ge(s_lin1, 1)
            pe.wait_ge(s_xb_zero, 1)
            for i in range(node_tiles):
                n0 = i * P
                if i in X_SPLIT:
                    pe.wait_ge(s_x[X_SPLIT.index(i)], 32)
                if i == UNIT_ROWS_AFTER:
                    pe.wait_ge(s_diag, 1)
                    nc.tensor.matmul(turned[:, 0:2 * n_units], ones[0:n_units, :], diag[:, :], start=True,
                                     stop=True).then_inc(s_rows, 1)
                if i >= 4:
                    pe.wait_ge(s_h_sb, i - 3)
                o = w_ps[i % 4]
                nc.tensor.matmul(o[:, 0:P], xa[:, n0:n0 + P], w_of((0, P), C_PA, P),
                                 start=True, stop=False, skip_group_check=True)
                nc.tensor.matmul(o[:, FEAT - P:FEAT], xb[:, n0:n0 + P], w_of((0, P), C_PB, P),
                                 start=False, stop=True, skip_group_check=True).then_inc(s_h_mm, 1)

            def hidden_half(k, half, first=False):
                a, b = HALVES[half]
                pe.wait_ge(s_edges[half], k * 16 + 16)
                if half or not first:
                    pe.wait_ge(s_hid, k * 2 + half)
                nc.tensor.matmul(hidden_ps[:, 0:b - a], w_of((0, P), C_W1, P), edges[:, a:b], start=True, stop=True)\
                  .then_inc(s_hid_mm, 1)

            def mlp(it, g):
                ab, ts = GROUPS[g]
                pe.wait_ge(s_split, it * 2 + (1 + g // 4))
                pe.wait_ge(s_prod, it * NG + (g + 5))
                for k, t in enumerate(ts):
                    for part in (w2_high, w2_low):
                        last = nc.tensor.matmul(w_ps[g % 4][:, k * W_COLS:(k + 1) * W_COLS],
                                                hidden_parts[:, ab * UNIT + t * P:ab * UNIT + (t + 1) * P],
                                                part[:, :], start=part is w2_high, stop=part is w2_low)
                last.then_inc(s_w, 1)

            def sum_group(it, g):
                ab, ts = GROUPS[g]
                if g % 4 == 0:
                    pe.wait_ge(s_sel, it * 2 + (1 + g // 4))
                if g < 2:
                    pe.wait_ge(s_copied[ab], it + 1)
                pe.wait_ge(s_prod, it * NG + (NG + g + 1))
                for k, t in enumerate(ts):
                    j = FIRST[g] + k
                    last = nc.tensor.matmul(sums_ps[ab][:, 0:PROD], selector[:, j * P:(j + 1) * P],
                                            products[:, g, k, :], start=(t == 0), stop=(t == TILES - 1))
                last.then_inc(s_agg, 1)

            def turn(it, u, last_b=False):
                pe.wait_ge(s_copied[u], it + 1)
                if last_b:
                    pe.wait_ge(s_hid, it * 2 + 2)
                else:
                    pe.wait_ge(s_added, it * 2 + (u + 2))
                to = last_turned_ps if last_b else turned_ps
                nc.tensor.transpose(to[:, 0:P], sums_sb[:, u, 0:2 * S_CH], ident[:, :])
                for i in range(3):
                    c0 = 2 * S_CH + i * 3 * V_CH
                    last = nc.tensor.transpose(to[0:3 * V_CH, (i + 1) * P:(i + 2) * P],
                                               sums_sb[:, u, c0:c0 + 3 * V_CH], ident[:, :])
                last.then_inc(s_turned, 1)

            hidden_half(0, 0, True)
            hidden_half(0, 1, True)
            pe.wait_ge(s_w2, 1)
            for g in range(3):
                mlp(0, g)
            pe.wait_ge(s_ctl, 1)
            n_it = pe.value_load(passes_i[0:1, pairs:pairs + 1], min_val=pairs, max_val=pairs * max_passes)
            with pe.Fori(0, n_it) as it:
                mlp(it, 3)
                turn(it, 0)
                mlp(it, 4)
                sum_group(it, 0)
                mlp(it, 5)
                hidden_half(it + 1, 0)
                turn(it, 1)
                mlp(it, 6)
                sum_group(it, 1)
                sum_group(it, 2)
                sum_group(it, 3)
                mlp(it, 7)
                hidden_half(it + 1, 1)
                sum_group(it, 4)
                mlp(it + 1, 0)
                sum_group(it, 5)
                sum_group(it, 6)
                mlp(it + 1, 1)
                mlp(it + 1, 2)
                sum_group(it, 7)
            turn(n_it, 0)
            turn(n_it, 1, last_b=True)

            pe.wait_ge(s_added, n_it * 2 + 4)
            pe.wait_ge(s_out_w, 1)
            pe.wait_ge(s_xsum, 4 * 16)
            for i in range(node_tiles):
                if i >= len(out_ps):
                    pe.wait_ge(s_yv, i - len(out_ps) + 1)
                o = out_ps[i % len(out_ps)]
                n0 = i * P
                sums = [sums_1[:, n0:n0 + P]]
                for c in range(3):
                    sums.append(sums_v[:, 2 * c * NN + n0:2 * c * NN + n0 + P])
                for k in range(3):
                    m0 = (5 - 2 * k) * NN + n0
                    sums.append(sums_v[0:3 * V_CH, m0:m0 + P])
                for t, (col, width) in enumerate(TERMS):
                    last = nc.tensor.matmul(o[:, col:col + width], sums[t],
                                            w_of((0, sums[t].shape[0]), TERM_AT[t], width), start=(t == 0),
                                            stop=(t == len(TERMS) - 1), skip_group_check=True)
                last.then_inc(s_fin, 1)


def kernel(x, src, dst, edge_attr_4, edge_attr_64, node_vec1, L0_gnn_lin1_ws, L0_gnn_lin1_wv, L0_gnn_fc_w1,
           L0_gnn_fc_w2, L0_gnn_sc_ws, L0_gnn_sc_wv, L0_gnn_lin2_ws, L0_gnn_lin2_wv):
    import concourse.bacc as bacc
    from concourse.bass_utils import run_bass_kernel_spmd

    arr = lambda a: np.ascontiguousarray(a)
    x, src, dst, e4, e64, a = map(arr, (x, src, dst, edge_attr_4, edge_attr_64, node_vec1))
    w1, w2 = arr(L0_gnn_fc_w1), arr(L0_gnn_fc_w2)
    l1s, l1v, scs, scv = map(arr, (L0_gnn_lin1_ws, L0_gnn_lin1_wv, L0_gnn_sc_ws, L0_gnn_sc_wv))
    l2s, l2v = map(arr, (L0_gnn_lin2_ws, L0_gnn_lin2_wv))
    n, e = x.shape[0], src.shape[0]
    tiles = math.ceil((n + 1) / P)
    NN = tiles * P
    pairs = math.ceil(e / (2 * UNIT))
    e_pad = pairs * 2 * UNIT

    def padded(v, fill=0):
        out = np.full((e_pad,) + v.shape[1:], fill, v.dtype)
        out[:e] = v
        return out

    def by_tile(v):
        v = v.reshape((pairs, 2, TILES, P) + v.shape[1:])
        v = np.stack([v[:, ab, t] for ab, t in ORDER], axis=1)
        return np.ascontiguousarray(np.swapaxes(v, 1, 2))

    src_t = by_tile(padded(src))
    dst_p = padded(dst, n)
    dst_t = np.ascontiguousarray(by_tile(dst_p).transpose(1, 0, 2)).reshape(P, pairs * SLOTS)
    attr_t = np.ascontiguousarray(by_tile(padded(e4)).transpose(1, 0, 2, 3)).reshape(P, pairs * PAIR_ATTR)
    attr_t = np.concatenate([attr_t, np.zeros((P, PAIR_ATTR), e4.dtype)], axis=1)
    edges = np.ascontiguousarray(padded(e64).reshape(pairs, 2, UNIT, HID).transpose(0, 1, 3, 2))\
        .reshape(pairs, 2 * HID, UNIT)

    vectors = x[:, S_CH:].reshape(n, V_CH, 3).transpose(2, 1, 0)
    xa = np.zeros((P, NN), x.dtype)
    xa[:S_CH, :n] = x[:, :S_CH].T
    xa[S_CH:, :n] = vectors[:2].reshape(2 * V_CH, n)
    xb = np.zeros((V_CH, NN), x.dtype)
    xb[:, :n] = vectors[2]
    node = np.zeros((NN,), a.dtype)
    node[:n] = a[:, 0]
    node = np.ascontiguousarray(node.reshape(tiles, P).T)

    w = np.zeros((P, W_PACK), w1.dtype)
    for u in (0, 1):
        w[u * HID:(u + 1) * HID, C_W1 + u * HID:C_W1 + (u + 1) * HID] = w1
        w[u * HID:(u + 1) * HID, C_W2:C_W2 + W_COLS] = w2
    w[:S_CH, C_PA:C_PA + S_CH] = l1s
    w[S_CH:S_CH + V_CH, C_PA + S_CH:C_PA + S_CH + V_CH] = l1v
    w[S_CH + V_CH:, C_PA + S_CH + V_CH:C_PA + P] = l1v
    w[3 * V_CH:, C_PB + P - V_CH:C_PB + P] = l1v

    def place(term, row, col, block):
        c = TERM_AT[term] + col - TERMS[term][0]
        w[row:row + block.shape[0], c:c + block.shape[1]] = block

    place(0, 0, OUT_S, l2s[:S_CH])
    place(0, S_CH, OUT_S, scs)
    for i in range(3):
        place(1 + i, 0, OUT_V[i], l2v[S_CH:S_CH + V_CH])
        place(1 + i, V_CH, OUT_S, l2s[S_CH:])
        place(1 + i, 2 * V_CH, OUT_V[CROSS[2 * i][3]], l2v[S_CH + V_CH:])
        place(1 + i, 3 * V_CH, OUT_V[i], scv)
        place(4 + i, 0, OUT_V[i], l2v[:S_CH])
        place(4 + i, 2 * V_CH, OUT_V[CROSS[5 - 2 * i][3]], l2v[S_CH + V_CH:])

    arrays = {"xa": xa, "xb": xb, "x": x, "src": src_t, "dst_tiles": dst_t,
              "dst_units": dst_p.reshape(pairs * 2, UNIT), "attr": attr_t, "edges": edges, "node": node, "weights": w}
    nc = bacc.Bacc("TRN2", target_bir_lowering=False, num_devices=1)
    args = [nc.dram_tensor(f"{k}_dram", v.shape, mybir.dt.from_np(v.dtype), kind="ExternalInput").ap()
            for k, v in arrays.items()]
    out = nc.dram_tensor("out_dram", x.shape, F32, kind="ExternalOutput").ap()
    build(nc, *args, out, n)
    r = run_bass_kernel_spmd(nc, [{f"{k}_dram": v for k, v in arrays.items()}], core_ids=[0])
    return r.results[0]["out_dram"]
```
